# Optimizing a Trainium2 kernel written in Bass

```python
import numpy as np
import jax
import jax.numpy as jnp

def _softmax(x, axis=-1):
    return jax.nn.softmax(x, axis=axis)

def _gelu(x):
    return jax.nn.gelu(x, approximate=True)

def _silu(x):
    return jax.nn.silu(x)

def _sigmoid(x):
    return jax.nn.sigmoid(x)

def _layernorm(x, axis=-1, eps=1e-05):
    m = jnp.mean(x, axis=axis, keepdims=True)
    v = jnp.var(x, axis=axis, keepdims=True)
    return (x - m) / jnp.sqrt(v + eps)

def _scatter_add(tgt, idx, src, axis=0):
    return tgt.at[idx].add(src)

def _segment_sum(src, seg, n):
    return jax.ops.segment_sum(src, seg, n)
kernel_name = 'mk_adj_resnorm_d2_adj_r2_c70108'

def setup_inputs(seed: int=0):
    np.random.seed(seed)
    _w = jnp.asarray

    def _rec_inputs():
        import jax
        import jax.numpy as jnp
        _gk = jax.random.key(seed)
        x = 7.22e-05 + 1 * jax.random.normal(jax.random.fold_in(_gk, 1), (16, 512, 128), jnp.float32)
        _w = (1.0 + jnp.arange(512, dtype=jnp.float32)) ** (-0.5)
        _w = _w / _w.mean()
        _pij = jnp.clip(0.015625 * _w[:, None] * _w[None, :], 0.0, 1.0)
        _a = jax.random.uniform(jax.random.fold_in(_gk, 2), (16, 512, 512)) < _pij
        _a = jnp.logical_or(_a, jnp.swapaxes(_a, -1, -2))
        _a = jnp.logical_or(_a, jnp.eye(512, dtype=bool))
        _af = _a.astype(jnp.float32)
        _af = _af * jax.random.uniform(jax.random.fold_in(_gk, 3), (16, 512, 512), jnp.float32, 0.05, 1)
        adj = _af
        _nm = jnp.ones((16, 512), dtype=bool)
        nodemask = jnp.where(_nm, 1.0, 0.0).astype(jnp.float32)
        return (x, adj, nodemask)
    x, adj, nodemask = _rec_inputs()

    def _L0_gnn_setup():
        import jax, jax.numpy as jnp
        import numpy as np
        B, N, F_IN, F_OUT = (32, 512, 128, 128)
        EPS = 1e-08
        key = jax.random.key(seed)
        k1, k2, k3 = jax.random.split(key, 3)
        x = jax.random.normal(k1, (B, N, F_IN), dtype=jnp.float32)
        adj = jax.random.uniform(k2, (B, N, N), dtype=jnp.float32)
        fan_in, fan_out = (2 * F_IN, F_OUT)
        limit = float(np.sqrt(6.0 / (fan_in + fan_out)))
        weight = jax.random.uniform(k3, (2 * F_IN, F_OUT), minval=-limit, maxval=limit, dtype=jnp.float32)
        bias = jnp.zeros((F_OUT,), dtype=jnp.float32)
        return {'x': x, 'adj': adj, 'weight': weight, 'bias': bias}
    _L0_gnn_all = _L0_gnn_setup()
    _L0_gnn_in = {k: v for k, v in _L0_gnn_all.items() if k in ('weight', 'bias')}
    del _L0_gnn_all

    def _L1_gnn_setup():
        import jax, jax.numpy as jnp
        import numpy as np
        B, N, D, C, L = (64, 256, 128, 128, 5)
        EDGE_P = 0.02

        def _gru_cell(m, h, w_ih, w_hh, b_ih, b_hh):
            gi = m @ w_ih.T + b_ih
            gh = h @ w_hh.T + b_hh
            i_r, i_z, i_n = jnp.split(gi, 3, axis=-1)
            h_r, h_z, h_n = jnp.split(gh, 3, axis=-1)
            r = jax.nn.sigmoid(i_r + h_r)
            z = jax.nn.sigmoid(i_z + h_z)
            n = jnp.tanh(i_n + r * h_n)
            return (1.0 - z) * n + z * h
        key = jax.random.key(seed)
        ks = jax.random.split(key, 8)
        x = jax.random.normal(ks[0], (B, N, D), dtype=jnp.float32)
        adj = (jax.random.uniform(ks[1], (B, N, N)) < EDGE_P).astype(jnp.float32)
        mask = jnp.ones((B, N), dtype=jnp.float32)
        s = 1.0 / np.sqrt(C).astype(np.float32)
        weight = jax.random.uniform(ks[2], (L, C, C), minval=-s, maxval=s, dtype=jnp.float32)
        w_ih = jax.random.uniform(ks[3], (3 * C, C), minval=-s, maxval=s, dtype=jnp.float32)
        w_hh = jax.random.uniform(ks[4], (3 * C, C), minval=-s, maxval=s, dtype=jnp.float32)
        b_ih = jax.random.uniform(ks[5], (3 * C,), minval=-s, maxval=s, dtype=jnp.float32)
        b_hh = jax.random.uniform(ks[6], (3 * C,), minval=-s, maxval=s, dtype=jnp.float32)
        return dict(x=x, adj=adj, mask=mask, weight=weight, w_ih=w_ih, w_hh=w_hh, b_ih=b_ih, b_hh=b_hh)
    _L1_gnn_all = _L1_gnn_setup()
    _L1_gnn_in = {k: v for k, v in _L1_gnn_all.items() if k in ('weight', 'w_ih', 'w_hh', 'b_ih', 'b_hh')}
    del _L1_gnn_all
    return {'x': x, 'adj': adj, 'nodemask': nodemask, 'L0_gnn_weight': _L0_gnn_in['weight'], 'L0_gnn_bias': _L0_gnn_in['bias'], 'L1_gnn_weight': _L1_gnn_in['weight'], 'L1_gnn_w_ih': _L1_gnn_in['w_ih'], 'L1_gnn_w_hh': _L1_gnn_in['w_hh'], 'L1_gnn_b_ih': _L1_gnn_in['b_ih'], 'L1_gnn_b_hh': _L1_gnn_in['b_hh']}

def reference(x, adj, nodemask, L0_gnn_weight, L0_gnn_bias, L1_gnn_weight, L1_gnn_w_ih, L1_gnn_w_hh, L1_gnn_b_ih, L1_gnn_b_hh):
    import jax
    import jax.numpy as jnp

    def _L0_gnn_ref(x, adj, weight, bias):
        import jax, jax.numpy as jnp
        import numpy as np
        B, N, F_IN, F_OUT = (32, 512, 128, 128)
        EPS = 1e-08
        adj_norm = adj / (jnp.sum(adj, axis=-1, keepdims=True) + EPS)
        h_neigh = jnp.einsum('bnm,bmf->bnf', adj_norm, x)
        h_concat = jnp.concatenate([x, h_neigh], axis=-1)
        h = jnp.einsum('bnk,ko->bno', h_concat, weight) + bias
        return jax.nn.relu(h)

    def _L1_gnn_ref(x, adj, mask, weight, w_ih, w_hh, b_ih, b_hh):
        import jax, jax.numpy as jnp
        import numpy as np
        B, N, D, C, L = (64, 256, 128, 128, 5)
        EDGE_P = 0.02

        def _gru_cell(m, h, w_ih, w_hh, b_ih, b_hh):
            gi = m @ w_ih.T + b_ih
            gh = h @ w_hh.T + b_hh
            i_r, i_z, i_n = jnp.split(gi, 3, axis=-1)
            h_r, h_z, h_n = jnp.split(gh, 3, axis=-1)
            r = jax.nn.sigmoid(i_r + h_r)
            z = jax.nn.sigmoid(i_z + h_z)
            n = jnp.tanh(i_n + r * h_n)
            return (1.0 - z) * n + z * h
        A = (adj != 0).astype(x.dtype)
        h = x
        for l in range(weight.shape[0]):
            m = jnp.einsum('bnd,de->bne', h, weight[l])
            agg = jnp.einsum('bij,bid->bjd', A, m)
            h = _gru_cell(agg, h, w_ih, w_hh, b_ih, b_hh)
        return h * mask[..., None]
    x = _layernorm(x + _L0_gnn_ref(x, adj, L0_gnn_weight, L0_gnn_bias), axis=-1)
    x = _layernorm(x + _L1_gnn_ref(x, adj, nodemask, L1_gnn_weight, L1_gnn_w_ih, L1_gnn_w_hh, L1_gnn_b_ih, L1_gnn_b_hh), axis=-1)
    return x

_drawn_inputs = setup_inputs


def setup_inputs(seed=0):
    import zlib

    import numpy as np

    out = dict(_drawn_inputs(seed))
    spreads = {'L0_gnn_bias': (0.0, 0.1)}
    factors = {}
    for name, (base, spread) in spreads.items():
        noise = np.random.default_rng([zlib.crc32(name.encode()), seed]).standard_normal(out[name].shape)
        drawn = base * np.exp(spread * noise) if base else spread * noise
        out[name] = jnp.asarray(drawn.astype(out[name].dtype))
    for name, factor in factors.items():
        out[name] = (out[name] * factor).astype(out[name].dtype)
    return out
```

```python
from contextlib import ExitStack

import concourse.bass as bass
from concourse import mybir

ALU = mybir.AluOpType
ACT = mybir.ActivationFunctionType
F32 = mybir.dt.float32
F32R = mybir.dt.float32r

P = 128
LAYERS = 5
SLOTS = 5
LN_EPS = 1e-5
ROW_EPS = 1e-8



def has_unit(n, slot, batches):
    return 0 <= n < batches if slot % 2 == 0 else 1 <= n <= batches


def count(batches, n, slot, among):
    return sum(
        has_unit(m, s, batches)
        for m in range(-1, n + 1)
        for s in among
        if m < n or s < slot
    )


class Window:

    def __init__(self, batches, first, trip=None):
        self.batches, self.first, self.trip = batches, first, trip
        self.parity = first % 2

    def value(self, of_number):
        start = of_number(self.first)
        if self.trip is None:
            return start
        return self.trip * (of_number(self.first + 2) - start) + start

    def unit(self, slot):
        return has_unit(self.first, slot, self.batches)

    def before_unit(self):
        return has_unit(self.first - 1, 4, self.batches)

    def prepares(self):
        return -1 <= self.first < self.batches - 1

    def finishes(self):
        return 1 <= self.first <= self.batches

    def units(self, slot):
        return self.value(lambda n: count(self.batches, n, slot, range(SLOTS)))

    def carried(self, slot):
        return self.value(lambda n: count(self.batches, n, slot, (0, 1, 2, 4)))

    def turned(self, slot):
        return self.value(lambda n: count(self.batches, n, slot, (1, 2, 3, 4)))

    def prepared(self, each, k):
        return self.value(lambda n: each * (n + 1) + k)

    def young(self, each, k):
        return self.value(lambda n: each * n + k)

    def finished(self, each, k):
        return self.value(lambda n: each * (n - 1) + k)

    def freed(self, each=1):
        return self.value(lambda n: each * n)

    def loaded(self, back):
        return self.value(lambda n: 16 * ((n + 1 - back) // 2 + 1))


def program(nc, x, adj, nodemask, w0, b0, wl, w_ih, w_hh, b_ih, b_hh, out):
    B, N, D = x.shape
    C = N // P
    G = 3
    assert D == P and N == 512 and wl.shape[0] == LAYERS and B % 2 == 0 and B >= 4

    with ExitStack() as ctx:
        def sb(name, shape, dtype=F32):
            return ctx.enter_context(nc.sbuf_tensor(name, shape, dtype))

        def bank(name):
            return ctx.enter_context(nc.psum_tensor(name, [P, 512], F32))

        def sem(name):
            return ctx.enter_context(nc.semaphore(name))

        ident = sb("ident", [P, P])
        zero_tile = sb("zero_tile", [P, P])
        minus_half = sb("minus_half", [P, C])
        small_rows = sb("small_rows", [P, P])
        small_cols = sb("small_cols", [P, P])
        mask_cols = small_cols[:, 0:B * C]
        bih_cols = small_cols[:, B * C:B * C + G]
        bhh_cols = small_cols[:, B * C + G:B * C + 2 * G]
        bias0 = sb("bias0", [P, D])
        rz_bias = sb("rz_bias", [P, 2])
        w0_rows = sb("w0_rows", [P, 2 * D])
        w0_hi = sb("w0_hi", [P, 2 * D], F32R)
        w0_lo = sb("w0_lo", [P, 2 * D], F32R)
        wih_rows = sb("wih_rows", [P, G, D])
        whh_rows = sb("whh_rows", [P, G, D])
        wl_rows = sb("wl_rows", [P, LAYERS, D])
        wih_t = sb("wih_t", [P, G * D])
        wl_t = sb("wl_t", [P, LAYERS * D])
        whh_hi = sb("whh_hi", [P, G * D], F32R)
        whh_lo = sb("whh_lo", [P, G * D], F32R)
        wc_hi = sb("wc_hi", [P, LAYERS, G * D], F32R)
        wc_lo = sb("wc_lo", [P, LAYERS, G * D], F32R)

        adj_in = [sb(f"adj_in{i}", [P, C, N]) for i in range(2)]
        x_in = [sb(f"x_in{i}", [P, C, D]) for i in range(2)]
        edges = [sb(f"edges{i}", [P, C, N], F32R) for i in range(2)]
        x1_kept = [sb(f"x1_kept{i}", [P, C, D]) for i in range(2)]
        h = [sb(f"h{i}", [P, N]) for i in range(2)]
        h_hi = [sb(f"h_hi{i}", [P, N], F32R) for i in range(2)]
        h_lo = [sb(f"h_lo{i}", [P, N], F32R) for i in range(2)]

        adjt_hi = sb("adjt_hi", [P, C, N], F32R)
        adjt_lo = sb("adjt_lo", [P, C, N], F32R)
        xt_hi = sb("xt_hi", [P, N], F32R)
        xt_lo = sb("xt_lo", [P, N], F32R)
        DY = D + 2
        y_hi = sb("y_hi", [P, C, DY], F32R)
        y_lo = sb("y_lo", [P, C, DY], F32R)
        own = sb("own", [P, C, D])
        row_sum = sb("row_sum", [P, C])
        row_inv = sb("row_inv", [P, C])
        mixed = sb("mixed", [P, C, D])
        pre1 = sb("pre1", [P, C, D])
        stats1 = sb("stats1", [P, C, 6])
        mv1 = sb("mv1", [P, C, 2])
        var1 = sb("var1", [P, C])
        rstd1 = sb("rstd1", [P, C])
        x1 = sb("x1", [P, C, D])

        tok_hi = sb("tok_hi", [P, N], F32R)
        tok_lo = sb("tok_lo", [P, N], F32R)
        agg_hi = sb("agg_hi", [P, N], F32R)
        agg_lo = sb("agg_lo", [P, N], F32R)
        r_gate = sb("r_gate", [P, N])
        z_gate = sb("z_gate", [P, N])
        r_hn = sb("r_hn", [P, N])
        n_pre = sb("n_pre", [P, N])
        n_gate = sb("n_gate", [P, N])
        z_h = sb("z_h", [P, N])
        zm1_n = sb("zm1_n", [P, N])

        pre2 = sb("pre2", [P, C, D])
        stats2 = sb("stats2", [P, C, 6])
        mv2 = sb("mv2", [P, C, 2])
        var2 = sb("var2", [P, C])
        rstd2 = sb("rstd2", [P, C])
        cent2 = sb("cent2", [P, C, D])
        y_out = sb("y_out", [P, C, D])

        ps_tok = bank("ps_tok")
        ps_hn, ps_r, ps_z, ps_in = bank("ps_hn"), bank("ps_r"), bank("ps_z"), bank("ps_in")
        ps_b = [bank(f"ps_b{i}") for i in range(3)]

        s_small = sem("s_small")
        s_weights = sem("s_weights")
        s_adj_in = [sem(f"s_adj_in{i}") for i in range(2)]
        s_x_in = [sem(f"s_x_in{i}") for i in range(2)]
        s_stored = sem("s_stored")
        s_const = sem("s_const")
        s_w_turned = sem("s_w_turned")
        s_w_act = sem("s_w_act")
        s_w_dve = sem("s_w_dve")
        s_w_prod = sem("s_w_prod")
        s_wc_hi = sem("s_wc_hi")
        s_wc_lo = sem("s_wc_lo")
        s_xt = sem("s_xt")
        s_xt_hi = sem("s_xt_hi")
        s_xt_lo = sem("s_xt_lo")
        s_adjt = sem("s_adjt")
        s_adjt_hi = sem("s_adjt_hi")
        s_adjt_lo = sem("s_adjt_lo")
        s_xw = sem("s_xw")
        s_y_hi = sem("s_y_hi")
        s_own = sem("s_own")
        s_mean = sem("s_mean")
        s_rinv = sem("s_rinv")
        s_mixed = sem("s_mixed")
        s_pre1 = sem("s_pre1")
        s_stats1 = sem("s_stats1")
        s_mv1 = sem("s_mv1")
        s_var1 = sem("s_var1")
        s_rstd1 = sem("s_rstd1")
        s_x1 = sem("s_x1")
        s_x1_kept = sem("s_x1_kept")
        s_x1_hi = sem("s_x1_hi")
        s_x1_lo = sem("s_x1_lo")
        s_x1t = sem("s_x1t")
        s_h0 = sem("s_h0")
        s_h0_hi = sem("s_h0_hi")
        s_h0_lo = sem("s_h0_lo")
        s_edges = sem("s_edges")
        s_tok = sem("s_tok")
        s_tok_hi = sem("s_tok_hi")
        s_tok_lo = sem("s_tok_lo")
        s_agg = sem("s_agg")
        s_agg_hi = sem("s_agg_hi")
        s_agg_lo = sem("s_agg_lo")
        s_r_sum = sem("s_r_sum")
        s_z_sum = sem("s_z_sum")
        s_in_sum = sem("s_in_sum")
        s_r = sem("s_r")
        s_z = sem("s_z")
        s_rhn = sem("s_rhn")
        s_npre = sem("s_npre")
        s_n = sem("s_n")
        s_zh = sem("s_zh")
        s_zm1n = sem("s_zm1n")
        s_h = sem("s_h")
        s_h_hi = sem("s_h_hi")
        s_h_lo = sem("s_h_lo")
        s_last = sem("s_last")
        s_end_read = sem("s_end_read")
        s_stats2 = sem("s_stats2")
        s_mv2 = sem("s_mv2")
        s_var2 = sem("s_var2")
        s_rstd2 = sem("s_rstd2")
        s_cent2 = sem("s_cent2")
        s_out = sem("s_out")

        def raw(ap):
            return ap.bitcast(F32)

        def all_windows(eng, window):
            window(Window(B, -1))
            window(Window(B, 0))
            with eng.Fori(0, (B - 2) // 2) as trip:
                window(Window(B, 1, trip))
                window(Window(B, 2, trip))
            window(Window(B, B - 1))
            window(Window(B, B))

        def state_of(w, slot):
            return w.parity if slot % 2 == 0 else 1 - w.parity

        def state_units(w, slot, counted):
            return counted(0) if slot == 1 else counted(slot - 1)

        block = ctx.enter_context(nc.Block())

        @block.sync
        def _(sp):
            def load(w, b, parity, wait):
                if wait:
                    sp.wait_ge(s_edges, w.value(lambda n: C * (n + 1)))
                    sp.wait_ge(s_pre1, w.value(lambda n: n + 1))
                sp.dma_start(x_in[parity][:], x[b].rearrange("(c p) d -> p c d", p=P)).then_inc(s_x_in[parity], 16)
                sp.dma_start(adj_in[parity][:], adj[b].rearrange("(c p) m -> p c m", p=P)).then_inc(s_adj_in[parity], 16)

            sp.sem_inc(s_stored, 16)
            first = Window(B, -1)
            load(first, 0, 0, False)
            sp.dma_start(w0_rows[:].rearrange("p (k d) -> p k d", k=2),
                         w0.rearrange("(k p) d -> p k d", p=P)).then_inc(s_small, 16)
            sp.dma_start(bias0[:], b0.partition_broadcast(P)).then_inc(s_small, 16)
            load(first, 1, 1, False)

            def window(w):
                if 0 <= w.first < B - 2:
                    sp_b = w.first + 2 if w.trip is None else w.trip * 2 + (w.first + 2)
                    load(w, sp_b, w.parity, True)
                if w.finishes():
                    sp.wait_ge(s_out, w.finished(1, 1))
                    b = w.first - 1 if w.trip is None else w.trip * 2 + (w.first - 1)
                    sp.dma_start(out[b].rearrange("(c p) d -> p c d", p=P), y_out[:]).then_inc(s_stored, 16)

            window(Window(B, 0))
            with sp.Fori(0, (B - 4) // 2) as trip:
                window(Window(B, 1, trip))
                window(Window(B, 2, trip))
            for n in range(B - 3, B + 1):
                window(Window(B, n))
            sp.wait_ge(s_stored, 16 * (B + 1))

        @block.gpsimd
        def _(pool):
            pool.sem_inc(s_cent2, 1)
            nc.gpsimd.memset(zero_tile[:], 0.0).then_inc(s_const, 1)
            nc.gpsimd.memset(minus_half[:], -0.5).then_inc(s_const, 1)
            nc.gpsimd.memset(raw(y_hi[:]), 1.0).then_inc(s_const, 1)
            nc.gpsimd.memset(raw(y_lo[:]), 0.0).then_inc(s_const, 1)
            nc.gpsimd.memset(small_rows[:], 0.0).then_inc(s_const, 1)
            pool.wait_ge(s_const, 5)
            nc.gpsimd.affine_select(out=ident[:], in_=zero_tile[:], compare_op=ALU.not_equal, fill=1.0, base=0,
                                    pattern=[[-1, P]], channel_multiplier=1).then_inc(s_const, 1)

            def unit_tail(w, slot, parity, last):
                pool.wait_ge(s_z, w.units(slot))
                nc.gpsimd.tensor_tensor(z_h[:], z_gate[:], h[parity][:], ALU.mult).then_inc(s_zh, 1)
                if not last:
                    pool.wait_ge(s_h_hi, w.carried(slot))
                    nc.gpsimd.tensor_tensor(h_lo[parity][:], h[parity][:], raw(h_hi[parity][:]),
                                            ALU.subtract).then_inc(s_h_lo, 1)

            def window(w):
                for slot in range(SLOTS):
                    if slot == 0 and w.before_unit():
                        unit_tail(w, 0, 1 - w.parity, False)
                    if slot > 0 and w.unit(slot - 1):
                        unit_tail(w, slot, state_of(w, slot - 1), slot - 1 == 3)
                    if slot == 3 and w.prepares():
                        pool.wait_ge(s_var1, w.prepared(1, 1))
                        nc.gpsimd.tensor_tensor(rstd1[:], var1[:], minus_half[:], ALU.pow).then_inc(s_rstd1, 1)
                    if slot == 4 and w.prepares():
                        pool.wait_ge(s_x1_hi, w.prepared(1, 1))
                        nc.gpsimd.tensor_tensor(tok_lo[:], x1[:].rearrange("p c d -> p (c d)"),
                                                raw(tok_hi[:]), ALU.subtract).then_inc(s_x1_lo, 1)
                        pool.wait_ge(s_h0_hi, w.prepared(1, 1))
                        nc.gpsimd.tensor_tensor(h_lo[1 - w.parity][:], h[1 - w.parity][:],
                                                raw(h_hi[1 - w.parity][:]), ALU.subtract).then_inc(s_h0_lo, 1)
                    if slot == 4 and w.finishes():
                        pool.wait_ge(s_var2, w.finished(1, 1))
                        nc.gpsimd.tensor_tensor(rstd2[:], var2[:], minus_half[:], ALU.pow).then_inc(s_rstd2, 1)
                        nc.gpsimd.tensor_tensor(cent2[:], pre2[:], mv2[:, :, 0:1].to_broadcast([P, C, D]),
                                                ALU.subtract).then_inc(s_cent2, 1)
                        pool.wait_ge(s_stored, w.freed(16))
                        pool.wait_ge(s_rstd2, w.finished(1, 1))
                        pool.wait_ge(s_cent2, w.finished(1, 2))
                        nc.gpsimd.tensor_tensor(y_out[:], cent2[:],
                                                rstd2[:].rearrange("p (c o) -> p c o", o=1).to_broadcast([P, C, D]),
                                                ALU.mult).then_inc(s_out, 1)
                    if slot == 4 and w.prepares():
                        nc.gpsimd.tensor_copy(x1_kept[1 - w.parity][:], x1[:]).then_inc(s_x1_kept, 1)

            all_windows(pool, window)

        @block.scalar
        def _(act):
            act.dma_start(wih_rows[:], w_ih.rearrange("(g p) d -> p g d", p=P)).then_inc(s_weights, 16)
            act.dma_start(wl_rows[:], wl.rearrange("l p d -> p l d")).then_inc(s_weights, 16)
            act.dma_start(whh_rows[:], w_hh.rearrange("(g p) d -> p g d", p=P)).then_inc(s_weights, 16)

            act.wait_ge(s_const, 5)
            act.dma_start(small_rows[0:B * C, :],
                           nodemask.rearrange("b (c p) -> (b c) p", p=P)).then_inc(s_small, 16)
            act.dma_start(small_rows[B * C:B * C + G, :],
                           b_ih.rearrange("(g p) -> g p", p=P)).then_inc(s_small, 16)
            act.dma_start(small_rows[B * C + G:B * C + 2 * G, :],
                           b_hh.rearrange("(g p) -> g p", p=P)).then_inc(s_small, 16)

            def evacuate(dst, src):
                return nc.scalar.activation(dst, src, ACT.Copy)

            act.wait_ge(s_w_turned, 1)
            evacuate(wih_t[:], ps_b[1][:, 0:G * D]).then_inc(s_w_act, 1)
            act.wait_ge(s_w_turned, 2)
            evacuate(wl_t[:, 0:4 * D], ps_r[:, 0:4 * D]).then_inc(s_w_act, 1)
            act.wait_ge(s_w_turned, 3)
            evacuate(wl_t[:, 4 * D:5 * D], ps_z[:, 0:D]).then_inc(s_w_act, 1)
            evacuate(small_cols[:], ps_z[:, D:D + P]).then_inc(s_w_act, 1)
            act.wait_ge(s_w_turned, 4)
            evacuate(whh_hi[:], ps_b[0][:, 0:G * D]).then_inc(s_w_act, 1)
            for l, bank_of in enumerate((ps_hn, ps_in, ps_tok, ps_b[2], ps_b[1])):
                act.wait_ge(s_w_prod, l + 1)
                evacuate(wc_hi[:, l, :], bank_of[:, 0:G * D]).then_inc(s_wc_hi, 1)

            def window(w):
                other = 1 - w.parity

                def adjt_hi_of(j, b):
                    act.wait_ge(s_adjt, w.prepared(C, j + 1))
                    evacuate(adjt_hi[:, j, :], ps_b[b][:]).then_inc(s_adjt_hi, 1)

                def y_hi_of(half):
                    act.wait_ge(s_xw, w.prepared(2, half + 1))
                    evacuate(y_hi[:, 2 * half:2 * half + 2, 0:D],
                             ps_b[half][:].rearrange("p (c k d) -> p c k d", c=2, k=2)[:, :, 1, :]).then_inc(s_y_hi, 1)

                for slot in range(SLOTS):
                    tail = w.before_unit() if slot == 0 else w.unit(slot - 1)
                    parity = other if slot == 0 else state_of(w, slot - 1)
                    if tail:
                        act.wait_ge(s_npre, w.units(slot))
                        nc.scalar.activation(n_gate[:], n_pre[:], ACT.Tanh,
                                             bias=bih_cols[:, 2:3]).then_inc(s_n, 1)
                    if w.unit(slot):
                        act.wait_ge(s_agg, w.units(slot + 1))
                        evacuate(agg_hi[:], ps_tok[:]).then_inc(s_agg_hi, 1)
                    if tail and slot != 4:
                        act.wait_ge(s_h, w.units(slot))
                        evacuate(h_hi[parity][:], h[parity][:]).then_inc(s_h_hi, 1)
                    if w.prepares():
                        if slot == 0:
                            act.wait_ge(s_xt, w.prepared(1, 1))
                            evacuate(xt_hi[:], ps_b[0][:]).then_inc(s_xt_hi, 1)
                            adjt_hi_of(0, 1)
                            adjt_hi_of(1, 2)
                        if slot == 1:
                            y_hi_of(0)
                            adjt_hi_of(2, 2)
                            y_hi_of(1)
                        if slot == 4:
                            if w.unit(4):
                                act.wait_ge(s_agg, w.units(5))
                            act.wait_ge(s_x1, w.prepared(C, C))
                            evacuate(tok_hi[:], x1[:].rearrange("p c d -> p (c d)")).then_inc(s_x1_hi, 1)
                    if slot < 4 and w.unit(slot + 1):
                        act.wait_ge(s_tok, w.turned(slot + 2))
                        evacuate(tok_hi[:], ps_tok[:]).then_inc(s_tok_hi, 1)
                    if w.unit(slot):
                        act.wait_ge(s_r_sum, w.units(slot + 1))
                        if w.first > 0 or slot > 0:
                            act.wait_ge(s_rhn, w.units(slot))
                        nc.scalar.activation(r_gate[:], ps_r[:], ACT.Sigmoid, bias=rz_bias[:, 0:1]).then_inc(s_r, 1)
                        act.wait_ge(s_z_sum, w.units(slot + 1))
                        if w.first > 0 or slot > 0:
                            act.wait_ge(s_h, w.units(slot))
                        nc.scalar.activation(z_gate[:], ps_z[:], ACT.Sigmoid, bias=rz_bias[:, 1:2]).then_inc(s_z, 1)
                    if w.prepares():
                        if slot == 1:
                            adjt_hi_of(3, 0)
                        if slot == 4:
                            act.wait_ge(s_x1t, w.prepared(1, 1))
                            evacuate(h[other][:], ps_b[0][:]).then_inc(s_h0, 1)
                            act.wait_ge(s_h0, w.prepared(1, 1))
                            evacuate(h_hi[other][:], h[other][:]).then_inc(s_h0_hi, 1)

            all_windows(act, window)

        @block.vector
        def _(dve):
            def low_part(dst, src, hi):
                return nc.vector.tensor_tensor(dst, src, raw(hi), ALU.subtract)

            dve.sem_inc(s_end_read, 1)
            dve.wait_ge(s_small, 5 * 16)
            nc.vector.tensor_copy(w0_hi[:], w0_rows[:]).then_inc(s_w_dve, 1)
            dve.wait_ge(s_w_dve, 1)
            low_part(w0_lo[:], w0_rows[:], w0_hi[:]).then_inc(s_w_dve, 1)
            dve.wait_ge(s_w_act, 4)
            nc.vector.tensor_tensor(rz_bias[:], bih_cols[:, 0:2], bhh_cols[:, 0:2], ALU.add).then_inc(s_w_dve, 1)
            dve.wait_ge(s_w_act, 5)
            low_part(whh_lo[:], ps_b[0][:, 0:G * D], whh_hi[:]).then_inc(s_w_dve, 1)
            for l, bank_of in enumerate((ps_hn, ps_in, ps_tok, ps_b[2], ps_b[1])):
                dve.wait_ge(s_wc_hi, l + 1)
                low_part(wc_lo[:, l, :], bank_of[:, 0:G * D], wc_hi[:, l, :]).then_inc(s_wc_lo, 1)

            def window(w):
                other = 1 - w.parity
                prev = w.units

                def adjt_lo_of(j, b):
                    dve.wait_ge(s_adjt_hi, w.prepared(C, j + 1))
                    low_part(adjt_lo[:, j, :], ps_b[b][:], adjt_hi[:, j, :]).then_inc(s_adjt_lo, 1)

                def xw_parts(half):
                    ps = ps_b[half][:].rearrange("p (c k d) -> p c k d", c=2, k=2)
                    dve.wait_ge(s_y_hi, w.prepared(2, half + 1))
                    low_part(y_lo[:, 2 * half:2 * half + 2, 0:D], ps[:, :, 1, :], y_hi[:, 2 * half:2 * half + 2, 0:D])
                    nc.vector.tensor_tensor(own[:, 2 * half:2 * half + 2, :], ps[:, :, 0, :],
                                            bias0[:].rearrange("p (o d) -> p o d", o=1).to_broadcast([P, 2, D]),
                                            ALU.add).then_inc(s_own, 1)

                def mean_parts(half):
                    ps = ps_b[1 + half][:, 0:2 * DY].rearrange("p (c e) -> p c e", c=2)
                    cs = slice(2 * half, 2 * half + 2)
                    dve.wait_ge(s_mean, w.prepared(2, half + 1))
                    nc.vector.tensor_scalar(row_sum[:, cs], ps[:, :, D], ROW_EPS, None, ALU.add).then_inc(s_rinv, 1)
                    dve.wait_ge(s_rinv, w.prepared(4, 2 * half + 1))
                    nc.vector.reciprocal(row_inv[:, cs], row_sum[:, cs]).then_inc(s_rinv, 1)
                    dve.wait_ge(s_rinv, w.prepared(4, 2 * half + 2))
                    for c in range(2):
                        last = nc.vector.scalar_tensor_tensor(
                            out=mixed[:, 2 * half + c, :], in0=ps[:, c, 0:D],
                            scalar=row_inv[:, 2 * half + c:2 * half + c + 1],
                            in1=own[:, 2 * half + c, :], op0=ALU.mult, op1=ALU.add)
                    last.then_inc(s_mixed, 1)

                def edges_of(cs):
                    for c in cs:
                        nc.vector.tensor_scalar(edges[other][:, c, :], adj_in[other][:, c, :], 0.0, None,
                                                ALU.not_equal).then_inc(s_edges, 1)

                for slot in range(SLOTS):
                    tail = w.before_unit() if slot == 0 else w.unit(slot - 1)
                    parity = other if slot == 0 else state_of(w, slot - 1)
                    if tail:
                        dve.wait_ge(s_in_sum, prev(slot))
                        dve.wait_ge(s_rhn, prev(slot))
                        nc.vector.tensor_tensor(n_pre[:], ps_in[:], r_hn[:], ALU.add).then_inc(s_npre, 1)
                    if w.prepares() and slot == 3:
                        mean_parts(1)
                    if w.prepares() and slot == 4:
                        dve.wait_ge(s_rstd1, w.prepared(1, 1))
                        for c in range(C):
                            nc.vector.tensor_scalar(x1[:, c, :], pre1[:, c, :], mv1[:, c, 0:1],
                                                    rstd1[:, c:c + 1], ALU.subtract, ALU.mult).then_inc(s_x1, 1)
                    if tail:
                        dve.wait_ge(s_n, prev(slot))
                        nc.vector.scalar_tensor_tensor(out=zm1_n[:], in0=z_gate[:], scalar=1.0, in1=n_gate[:],
                                                       op0=ALU.subtract, op1=ALU.mult).then_inc(s_zm1n, 1)
                        dve.wait_ge(s_zh, prev(slot))
                        dve.wait_ge(s_zm1n, prev(slot))
                        nc.vector.tensor_tensor(h[parity][:], z_h[:], zm1_n[:], ALU.subtract).then_inc(s_h, 1)
                    if w.unit(slot):
                        dve.wait_ge(s_agg_hi, prev(slot + 1))
                        low_part(agg_lo[:], ps_tok[:], agg_hi[:]).then_inc(s_agg_lo, 1)
                    if w.prepares():
                        if slot == 0:
                            dve.wait_ge(s_xt_hi, w.prepared(1, 1))
                            low_part(xt_lo[:], ps_b[0][:], xt_hi[:]).then_inc(s_xt_lo, 1)
                            adjt_lo_of(0, 1)
                        if slot == 1:
                            xw_parts(0)
                            adjt_lo_of(2, 2)
                        if slot == 3:
                            dve.wait_ge(s_mixed, w.prepared(2, 2))
                            nc.vector.scalar_tensor_tensor(out=pre1[:], in0=mixed[:], scalar=0.0,
                                                           in1=x_in[other][:], op0=ALU.max,
                                                           op1=ALU.add).then_inc(s_pre1, 1)
                            dve.wait_ge(s_pre1, w.prepared(1, 1))
                            for c in range(C):
                                nc.vector.bn_stats(stats1[:, c, :], pre1[:, c, :]).then_inc(s_stats1, 1)
                            if w.unit(3):
                                dve.wait_ge(s_agg, prev(4))
                            dve.wait_ge(s_stats1, w.prepared(C, C))
                            edges_of((0,))
                            for c in range(C):
                                nc.vector.bn_aggr(mv1[:, c, :], stats1[:, c, :]).then_inc(s_mv1, 1)
                            dve.wait_ge(s_mv1, w.prepared(C, C))
                            nc.vector.tensor_scalar(var1[:], mv1[:, :, 1], LN_EPS, None, ALU.add).then_inc(s_var1, 1)
                    if slot < 4 and w.unit(slot + 1):
                        dve.wait_ge(s_tok_hi, w.turned(slot + 2))
                        low_part(tok_lo[:], ps_tok[:], tok_hi[:]).then_inc(s_tok_lo, 1)
                    if w.prepares():
                        if slot == 0:
                            adjt_lo_of(1, 2)
                        if slot == 1:
                            xw_parts(1)
                        if slot == 3:
                            edges_of((1, 2, 3))
                    if slot == 4 and w.finishes():
                        dve.wait_ge(s_last, w.finished(1, 1))
                        dve.wait_ge(s_x1_kept, w.value(lambda n: n))
                        dve.wait_ge(s_cent2, w.freed())
                        b = w.first - 1 if w.trip is None else w.trip * 2 + (w.first - 1)
                        for c in range(C):
                            last = nc.vector.scalar_tensor_tensor(
                                out=pre2[:, c, :], in0=ps_tok[:, c * P:(c + 1) * P],
                                scalar=mask_cols[:, bass.ds(b * C + c, 1)],
                                in1=x1_kept[other][:, c, :], op0=ALU.mult, op1=ALU.add)
                        last.then_inc(s_end_read, 1)
                        dve.wait_ge(s_end_read, w.finished(1, 2))
                        for c in range(C):
                            nc.vector.bn_stats(stats2[:, c, :], pre2[:, c, :]).then_inc(s_stats2, 1)
                    if slot == 4 and w.finishes():
                        dve.wait_ge(s_stats2, w.finished(C, C))
                    if w.unit(slot):
                        dve.wait_ge(s_r, prev(slot + 1))
                        nc.vector.scalar_tensor_tensor(out=r_hn[:], in0=ps_hn[:], scalar=bhh_cols[:, 2:3],
                                                       in1=r_gate[:], op0=ALU.add, op1=ALU.mult).then_inc(s_rhn, 1)
                    if w.prepares():
                        if slot == 1:
                            adjt_lo_of(3, 0)
                        if slot == 2:
                            mean_parts(0)
                    if slot == 4 and w.finishes():
                        for c in range(C):
                            nc.vector.bn_aggr(mv2[:, c, :], stats2[:, c, :]).then_inc(s_mv2, 1)
                        dve.wait_ge(s_mv2, w.finished(C, C))
                        nc.vector.tensor_scalar(var2[:], mv2[:, :, 1], LN_EPS, None, ALU.add).then_inc(s_var2, 1)

            all_windows(dve, window)

        @block.tensor
        def _(pe):
            def turn(dst, src):
                return nc.tensor.transpose(dst, src, ident[:])

            def split_product(dst, lhs_hi, lhs_lo, rhs_hi, rhs_lo, start, stop):
                nc.tensor.matmul(dst, lhs_hi, rhs_hi, start=start, stop=False)
                nc.tensor.matmul(dst, lhs_hi, rhs_lo, start=False, stop=False)
                return nc.tensor.matmul(dst, lhs_lo, rhs_hi, start=False, stop=stop)

            pe.wait_ge(s_const, 6)
            pe.wait_ge(s_weights, 3 * 16)
            for g in range(G):
                last = turn(ps_b[1][:, g * D:(g + 1) * D], wih_rows[:, g, :])
            last.then_inc(s_w_turned, 1)
            for l in range(4):
                last = turn(ps_r[:, l * D:(l + 1) * D], wl_rows[:, l, :])
            last.then_inc(s_w_turned, 1)
            pe.wait_ge(s_small, 5 * 16)
            turn(ps_z[:, 0:D], wl_rows[:, 4, :])
            turn(ps_z[:, D:2 * D], small_rows[:]).then_inc(s_w_turned, 1)
            for g in range(G):
                last = turn(ps_b[0][:, g * D:(g + 1) * D], whh_rows[:, g, :])
            last.then_inc(s_w_turned, 1)
            pe.wait_ge(s_w_act, 4)
            for l, bank_of in enumerate((ps_hn, ps_in, ps_tok, ps_b[2], ps_b[1])):
                nc.tensor.matmul(bank_of[:, 0:G * D], wl_t[:, l * D:(l + 1) * D], wih_t[:],
                                 start=True, stop=True).then_inc(s_w_prod, 1)
            pe.wait_ge(s_wc_lo, LAYERS)
            pe.wait_ge(s_w_dve, 4)

            def window(w):
                other = 1 - w.parity

                def turn_adj(j, b):
                    for i in range(C):
                        last = turn(ps_b[b][:, i * P:(i + 1) * P], adj_in[other][:, i, j * P:(j + 1) * P])
                    last.then_inc(s_adjt, 1)

                def own_products(half):
                    for c in range(2):
                        ts = slice((2 * half + c) * P, (2 * half + c + 1) * P)
                        last = split_product(ps_b[half][:, c * 2 * D:(c + 1) * 2 * D], xt_hi[:, ts], xt_lo[:, ts],
                                             w0_hi[:], w0_lo[:], True, True)
                    last.then_inc(s_xw, 1)

                def neighbour_sums(half):
                    for c in range(2):
                        i = 2 * half + c
                        ts = slice(i * P, (i + 1) * P)
                        for j in range(C):
                            last = split_product(ps_b[1 + half][:, c * DY:(c + 1) * DY], adjt_hi[:, j, ts],
                                                 adjt_lo[:, j, ts], y_hi[:, j, :], y_lo[:, j, :],
                                                 j == 0, j == C - 1)
                    last.then_inc(s_mean, 1)

                def gate(dst, g, hi, lo, weights_hi, weights_lo, start, stop):
                    gs = slice(g * D, (g + 1) * D)
                    return split_product(dst[:], weights_hi[:, gs], weights_lo[:, gs], hi[:], lo[:], start, stop)

                for slot in range(SLOTS):
                    unit = w.unit(slot)
                    s = state_of(w, slot)
                    layer = (0, 3, 1, 4, 2)[slot]
                    if unit:
                        if slot == 0:
                            pe.wait_ge(s_x1_lo, w.young(1, 1))
                            pe.wait_ge(s_edges, w.young(C, C))
                            if w.first > 0:
                                pe.wait_ge(s_end_read, w.freed())
                        else:
                            pe.wait_ge(s_tok_lo, w.turned(slot + 1))
                        for c in range(C):
                            ts = slice(c * P, (c + 1) * P)
                            nc.tensor.matmul(ps_tok[:], tok_hi[:, ts], edges[s][:, c, :], start=c == 0, stop=False)
                            last = nc.tensor.matmul(ps_tok[:], tok_lo[:, ts], edges[s][:, c, :],
                                                    start=False, stop=c == C - 1)
                        last.then_inc(s_agg, 1)
                    if w.prepares():
                        if slot == 0:
                            pe.wait_ge(s_x_in[other], w.loaded(0))
                            if w.first >= 0:
                                pe.wait_ge(s_h0, w.prepared(1, 0))
                            for c in range(C):
                                last = turn(ps_b[0][:, c * P:(c + 1) * P], x_in[other][:, c, :])
                            last.then_inc(s_xt, 1)
                            pe.wait_ge(s_adj_in[other], w.loaded(0))
                            if w.first >= 0:
                                pe.wait_ge(s_mixed, w.prepared(2, 0))
                            turn_adj(0, 1)
                            turn_adj(1, 2)
                        if slot == 1:
                            pe.wait_ge(s_xt_lo, w.prepared(1, 1))
                            own_products(0)
                            pe.wait_ge(s_adjt_lo, w.prepared(C, 2))
                            turn_adj(2, 2)
                            own_products(1)
                        if slot == 2:
                            pe.wait_ge(s_own, w.prepared(2, 2))
                            pe.wait_ge(s_adjt_lo, w.prepared(C, C))
                            neighbour_sums(0)
                            neighbour_sums(1)
                    if unit:
                        if slot == 0:
                            pe.wait_ge(s_h0_lo, w.young(1, 1))
                        else:
                            pe.wait_ge(s_h_lo, state_units(w, slot, w.carried))
                        started = w.first > 0 or slot > 0
                        if started:
                            pe.wait_ge(s_rhn, w.units(slot))
                        gate(ps_hn, 2, h_hi[s], h_lo[s], whh_hi, whh_lo, True, True)
                        if started:
                            pe.wait_ge(s_z, w.units(slot))
                        gate(ps_r, 0, h_hi[s], h_lo[s], whh_hi, whh_lo, True, False)
                        gate(ps_z, 1, h_hi[s], h_lo[s], whh_hi, whh_lo, True, False)
                        pe.wait_ge(s_agg_lo, w.units(slot + 1))
                    if slot < 4 and w.unit(slot + 1):
                        t = state_of(w, slot + 1)
                        if slot == 0 and not unit:
                            pe.wait_ge(s_end_read, w.freed())
                        pe.wait_ge(s_h, state_units(w, slot + 1, w.units))
                        for c in range(C):
                            last = turn(ps_tok[:, c * P:(c + 1) * P], h[t][:, c * P:(c + 1) * P])
                        last.then_inc(s_tok, 1)
                    if slot == 4 and w.finishes():
                        pe.wait_ge(s_h, w.units(4))
                        for c in range(C):
                            last = turn(ps_tok[:, c * P:(c + 1) * P], h[other][:, c * P:(c + 1) * P])
                        last.then_inc(s_last, 1)
                    if w.prepares():
                        if slot == 1:
                            pe.wait_ge(s_own, w.prepared(2, 1))
                            turn_adj(3, 0)
                        if slot == 4:
                            pe.wait_ge(s_x1, w.prepared(C, C))
                            for c in range(C):
                                last = turn(ps_b[0][:, c * P:(c + 1) * P], x1[:, c, :])
                            last.then_inc(s_x1t, 1)
                    if unit:
                        wi_hi, wi_lo = wc_hi[:, layer, :], wc_lo[:, layer, :]
                        gate(ps_r, 0, agg_hi, agg_lo, wi_hi, wi_lo, False, True).then_inc(s_r_sum, 1)
                        gate(ps_z, 1, agg_hi, agg_lo, wi_hi, wi_lo, False, True).then_inc(s_z_sum, 1)
                        if started:
                            pe.wait_ge(s_npre, w.units(slot))
                        gate(ps_in, 2, agg_hi, agg_lo, wi_hi, wi_lo, True, True).then_inc(s_in_sum, 1)

            all_windows(pe, window)


_INS = ["x", "adj", "nodemask", "L0_gnn_weight", "L0_gnn_bias", "L1_gnn_weight", "L1_gnn_w_ih", "L1_gnn_w_hh",
        "L1_gnn_b_ih", "L1_gnn_b_hh"]


def kernel(**inputs):
    import numpy as _np
    import concourse.bacc as _bacc
    from concourse import mybir as _mybir
    from concourse.bass_utils import run_bass_kernel_spmd as _run

    nc = _bacc.Bacc("TRN2", target_bir_lowering=False, num_devices=1)
    arrays, args = {}, []
    for name in _INS:
        a = _np.ascontiguousarray(inputs[name])
        arrays[f"in_{name}_dram"] = a
        args.append(nc.dram_tensor(f"in_{name}_dram", a.shape, _mybir.dt.from_np(a.dtype), kind="ExternalInput").ap())
    shape = tuple(inputs["x"].shape)
    args.append(nc.dram_tensor("out_dram", shape, _mybir.dt.float32, kind="ExternalOutput").ap())
    program(nc, *args)
    return _run(nc, [arrays], core_ids=[0]).results[0]["out_dram"]
```

```python
from contextlib import ExitStack

import concourse.bass as bass
from concourse import mybir

ALU = mybir.AluOpType
ACT = mybir.ActivationFunctionType
F32 = mybir.dt.float32
F32R = mybir.dt.float32r

P = 128
LAYERS = 5
SLOTS = 5
LN_EPS = 1e-5
ROW_EPS = 1e-8

UNITS = ((0, 0), (1, 2), (2, 4), (0, 1), (1, 3))
SLOTS = len(UNITS)
LAST = 2


def has_unit(batches, n, slot):
    return 0 <= n - UNITS[slot][0] < batches


def count(batches, n, slot, among):
    return sum(
        has_unit(batches, m, s)
        for m in range(0, n + 1)
        for s in among
        if m < n or s < slot
    )


class Window:

    def __init__(self, batches, first, trip=None):
        self.batches, self.first, self.trip = batches, first, trip

    def value(self, of_number):
        start = of_number(self.first)
        if self.trip is None:
            return start
        return self.trip * (of_number(self.first + 1) - start) + start

    def batch(self, back):
        return self.value(lambda n: n - back)

    def unit(self, slot):
        return has_unit(self.batches, self.first, slot)

    def unit_before(self, slot):
        if slot == 0:
            return has_unit(self.batches, self.first - 1, SLOTS - 1)
        return self.unit(slot - 1)

    def prepares(self):
        return -1 <= self.first < self.batches - 1

    def finishes(self):
        return 3 <= self.first < self.batches + 3

    def loads(self):
        return -1 <= self.first < self.batches - 2

    def units(self, slot, among=range(SLOTS)):
        return self.value(lambda n: count(self.batches, n, slot, among))

    def carried(self, slot):
        return self.units(slot, [s for s in range(SLOTS) if s != LAST])

    def turned(self, slot):
        return self.units(slot, range(1, SLOTS))

    def until_made(self, slot, counted):
        back, layer = UNITS[slot]
        before = UNITS.index((back, layer - 1)) if (back, layer - 1) in UNITS else None
        if before is not None and before < slot:
            return counted(before + 1)
        before = UNITS.index((back - 1, layer - 1))
        shifted = Window(self.batches, self.first - 1, self.trip)
        return shifted.carried(before + 1) if counted == self.carried else shifted.units(before + 1)

    def prepared(self, each, k):
        return self.value(lambda n: each * (n + 1) + k)

    def young(self, each, k):
        return self.value(lambda n: each * n + k)

    def finished(self, each, k):
        return self.value(lambda n: each * (n - 3) + k)

    def freed(self, each=1):
        return self.value(lambda n: each * (n - 2))

    def last_layers(self):
        return self.value(lambda n: count(self.batches, n - 1, LAST + 1, range(SLOTS)))


def program(nc, x, xt, adj, adjt, mask, w0, b0, wlt, wiht, whht, bih, bhh, out):
    B, N, D = x.shape
    C = N // P
    G = 3
    assert D == P and N == 512 and wlt.shape[0] == LAYERS and B >= 6

    with ExitStack() as ctx:
        def sb(name, shape, dtype=F32):
            return ctx.enter_context(nc.sbuf_tensor(name, shape, dtype))

        def bank(name):
            return ctx.enter_context(nc.psum_tensor(name, [P, 512], F32))

        def sem(name):
            return ctx.enter_context(nc.semaphore(name))

        ident = sb("ident", [P, P])
        zero_tile = sb("zero_tile", [P, P])
        minus_half = sb("minus_half", [P, C])
        mask_cols = sb("mask_cols", [P, B * C])
        bias0 = sb("bias0", [P, D])
        bih_cols = sb("bih_cols", [P, G])
        bhh_cols = sb("bhh_cols", [P, G])
        rz_bias = sb("rz_bias", [P, 2])
        w0_in = sb("w0_in", [P, 2 * D])
        w0_hi = sb("w0_hi", [P, 2 * D], F32R)
        w0_lo = sb("w0_lo", [P, 2 * D], F32R)
        wih_t = sb("wih_t", [P, G * D])
        whh_t = sb("whh_t", [P, G * D])
        wl_t = sb("wl_t", [P, LAYERS, D])
        whh_hi = sb("whh_hi", [P, G * D], F32R)
        whh_lo = sb("whh_lo", [P, G * D], F32R)
        wc_hi = sb("wc_hi", [P, LAYERS, G * D], F32R)
        wc_lo = sb("wc_lo", [P, LAYERS, G * D], F32R)

        adj_in = sb("adj_in", [P, C, N])
        adjt_in = sb("adjt_in", [P, C, N])
        xt_in = sb("xt_in", [P, N])
        x_in = sb("x_in", [P, C, D])
        RING, KEPT = 3, 4
        edges = sb("edges", [P, RING, C, N], F32R)
        x1_kept = sb("x1_kept", [P, KEPT, C, D])
        h = [sb(f"h{i}", [P, N]) for i in range(LAYERS + 1)]
        h_hi = [sb(f"h_hi{i}", [P, N], F32R) for i in range(LAYERS)]
        h_lo = [sb(f"h_lo{i}", [P, N], F32R) for i in range(LAYERS)]

        adjt_hi = sb("adjt_hi", [P, C, N], F32R)
        adjt_lo = sb("adjt_lo", [P, C, N], F32R)
        xt_hi = sb("xt_hi", [P, N], F32R)
        xt_lo = sb("xt_lo", [P, N], F32R)
        y_hi = sb("y_hi", [P, C, D], F32R)
        y_lo = sb("y_lo", [P, C, D], F32R)
        own = sb("own", [P, C, D])
        sum_of = sb("sum_of", [P, C, N])
        mean_t = sb("mean_t", [P, N])
        row_sum = sb("row_sum", [P, C])
        row_eps = sb("row_eps", [P, C])
        row_inv = sb("row_inv", [P, C])
        mixed = sb("mixed", [P, C, D])
        pre1 = sb("pre1", [P, C, D])
        stats1 = sb("stats1", [P, C, 6])
        mv1 = sb("mv1", [P, C, 2])
        var1 = sb("var1", [P, C])
        rstd1 = sb("rstd1", [P, C])
        x1 = sb("x1", [P, C, D])

        tok_hi = sb("tok_hi", [P, N], F32R)
        tok_lo = sb("tok_lo", [P, N], F32R)
        agg_hi = sb("agg_hi", [P, N], F32R)
        agg_lo = sb("agg_lo", [P, N], F32R)
        r_gate = sb("r_gate", [P, N])
        z_gate = sb("z_gate", [P, N])
        r_hn = sb("r_hn", [P, N])
        n_pre = sb("n_pre", [P, N])
        n_gate = sb("n_gate", [P, N])
        z_h = sb("z_h", [P, N])
        zm1_n = sb("zm1_n", [P, N])

        pre2 = sb("pre2", [P, C, D])
        stats2 = sb("stats2", [P, C, 6])
        mv2 = sb("mv2", [P, C, 2])
        var2 = sb("var2", [P, C])
        rstd2 = sb("rstd2", [P, C])
        cent2 = sb("cent2", [P, C, D])
        y_out = sb("y_out", [P, C, D])

        ps_tok = bank("ps_tok")
        ps_hn, ps_r, ps_z, ps_in = bank("ps_hn"), bank("ps_r"), bank("ps_z"), bank("ps_in")
        ps_b = [bank(f"ps_b{i}") for i in range(3)]

        s_small = sem("s_small")
        s_weights = sem("s_weights")
        s_adj_in = sem("s_adj_in")
        s_adjt_in = sem("s_adjt_in")
        s_x_in = sem("s_x_in")
        s_xt_in = sem("s_xt_in")
        s_stored = sem("s_stored")
        s_const = sem("s_const")
        s_w0 = sem("s_w0")
        s_whh = sem("s_whh")
        s_w_prod = sem("s_w_prod")
        s_wc_hi = sem("s_wc_hi")
        s_wc_lo = sem("s_wc_lo")
        s_xt_hi = sem("s_xt_hi")
        s_xt_lo = sem("s_xt_lo")
        s_adjt_hi = sem("s_adjt_hi")
        s_adjt_lo = sem("s_adjt_lo")
        s_row_sum = sem("s_row_sum")
        s_rinv = sem("s_rinv")
        s_xw = sem("s_xw")
        s_y_hi = sem("s_y_hi")
        s_own = sem("s_own")
        s_nsum = sem("s_nsum")
        s_nsum_out = sem("s_nsum_out")
        s_nsum_tok = sem("s_nsum_tok")
        s_mixed = sem("s_mixed")
        s_pre1 = sem("s_pre1")
        s_stats1 = sem("s_stats1")
        s_mv1 = sem("s_mv1")
        s_var1 = sem("s_var1")
        s_rstd1 = sem("s_rstd1")
        s_x1 = sem("s_x1")
        s_x1_kept = sem("s_x1_kept")
        s_x1_hi = sem("s_x1_hi")
        s_x1_lo = sem("s_x1_lo")
        s_x1t = sem("s_x1t")
        s_h0 = sem("s_h0")
        s_h0_hi = sem("s_h0_hi")
        s_h0_lo = sem("s_h0_lo")
        s_edges = sem("s_edges")
        s_tok = sem("s_tok")
        s_tok_hi = sem("s_tok_hi")
        s_tok_lo = sem("s_tok_lo")
        s_agg = sem("s_agg")
        s_agg_hi = sem("s_agg_hi")
        s_agg_lo = sem("s_agg_lo")
        s_r_sum = sem("s_r_sum")
        s_z_sum = sem("s_z_sum")
        s_in_sum = sem("s_in_sum")
        s_r = sem("s_r")
        s_z = sem("s_z")
        s_rhn = sem("s_rhn")
        s_npre = sem("s_npre")
        s_n = sem("s_n")
        s_zh = sem("s_zh")
        s_zm1n = sem("s_zm1n")
        s_h = sem("s_h")
        s_h_hi = sem("s_h_hi")
        s_h_lo = sem("s_h_lo")
        s_last = sem("s_last")
        s_end_read = sem("s_end_read")
        s_stats2 = sem("s_stats2")
        s_mv2 = sem("s_mv2")
        s_var2 = sem("s_var2")
        s_rstd2 = sem("s_rstd2")
        s_cent2 = sem("s_cent2")
        s_out = sem("s_out")

        def raw(ap):
            return ap.bitcast(F32)

        def all_windows(window, eng):
            for n in range(-1, 3):
                window(Window(B, n))
            with eng.Fori(0, B - 4) as trip:
                window(Window(B, 3, trip))
            for n in range(B - 1, B + 3):
                window(Window(B, n))

        product_bank = (ps_hn, ps_in, ps_tok, ps_r, ps_z)

        block = ctx.enter_context(nc.Block())

        @block.sync
        def _(sp):
            def load_xt(b):
                sp.dma_start(xt_in[:], xt[b]).then_inc(s_xt_in, 16)

            def load_adjt(b):
                sp.dma_start(adjt_in[:], adjt[b].rearrange("(c p) m -> p c m", p=P)).then_inc(s_adjt_in, 16)

            def load_x(b):
                sp.dma_start(x_in[:], x[b].rearrange("(c p) d -> p c d", p=P)).then_inc(s_x_in, 16)

            def load_adj(b):
                sp.dma_start(adj_in[:], adj[b].rearrange("(c p) m -> p c m", p=P)).then_inc(s_adj_in, 16)

            sp.sem_inc(s_stored, 16)
            load_xt(0)
            sp.dma_start(w0_in[:].rearrange("p (k d) -> p k d", k=2),
                         w0.rearrange("(k p) d -> p k d", p=P)).then_inc(s_w0, 16)
            load_adjt(0)
            load_adj(0)
            load_x(0)

            def window(w):
                if w.loads():
                    b = w.batch(-2)
                    sp.wait_ge(s_xt_lo, w.prepared(1, 1))
                    load_xt(b)
                    sp.wait_ge(s_adjt_lo, w.prepared(C, C))
                    load_adjt(b)
                if w.finishes():
                    sp.wait_ge(s_out, w.finished(1, 1))
                    sp.dma_start(out[w.batch(3)].rearrange("(c p) d -> p c d", p=P), y_out[:]).then_inc(s_stored, 16)
                if w.loads():
                    b = w.batch(-2)
                    sp.wait_ge(s_pre1, w.prepared(1, 1))
                    load_x(b)
                    sp.wait_ge(s_row_sum, w.prepared(C, C))
                    sp.wait_ge(s_edges, w.prepared(C, C))
                    load_adj(b)

            for n in range(-1, 3):
                window(Window(B, n))
            with sp.Fori(0, B - 5) as trip:
                window(Window(B, 3, trip))
            for n in range(B - 2, B + 3):
                window(Window(B, n))
            sp.wait_ge(s_stored, 16 * (B + 1))

        @block.gpsimd
        def _(pool):
            pool.sem_inc(s_cent2, 1)
            nc.gpsimd.memset(zero_tile[:], 0.0).then_inc(s_const, 1)
            nc.gpsimd.memset(minus_half[:], -0.5).then_inc(s_const, 1)
            pool.wait_ge(s_const, 2)
            nc.gpsimd.affine_select(out=ident[:], in_=zero_tile[:], compare_op=ALU.not_equal, fill=1.0, base=0,
                                    pattern=[[-1, P]], channel_multiplier=1).then_inc(s_const, 1)

            def window(w):

                def adjt_lo_of(j):
                    pool.wait_ge(s_adjt_hi, w.prepared(C, j + 1))
                    nc.gpsimd.tensor_tensor(adjt_lo[:, j, :], adjt_in[:, j, :], raw(adjt_hi[:, j, :]),
                                            ALU.subtract).then_inc(s_adjt_lo, 1)

                for slot in range(SLOTS):
                    made = UNITS[slot - 1][1] + 1
                    layer = UNITS[slot][1]
                    if w.prepares():
                        if slot == 0:
                            adjt_lo_of(0)
                            adjt_lo_of(1)
                        if slot == 1:
                            adjt_lo_of(2)
                            adjt_lo_of(3)
                        if slot == 4:
                            pool.wait_ge(s_x1_hi, w.prepared(1, 1))
                            nc.gpsimd.tensor_tensor(tok_lo[:], x1[:].rearrange("p c d -> p (c d)"),
                                                    raw(tok_hi[:]), ALU.subtract).then_inc(s_x1_lo, 1)
                    if w.prepares() and slot == 3:
                        pool.wait_ge(s_var1, w.prepared(1, 1))
                        nc.gpsimd.tensor_tensor(rstd1[:], var1[:], minus_half[:], ALU.pow).then_inc(s_rstd1, 1)
                    if slot == 2 and w.finishes():
                        pool.wait_ge(s_stored, w.freed(16))
                        pool.wait_ge(s_var2, w.finished(1, 1))
                        nc.gpsimd.tensor_tensor(rstd2[:], var2[:], minus_half[:], ALU.pow).then_inc(s_rstd2, 1)
                        nc.gpsimd.tensor_tensor(cent2[:], pre2[:], mv2[:, :, 0:1].to_broadcast([P, C, D]),
                                                ALU.subtract).then_inc(s_cent2, 1)
                        pool.wait_ge(s_rstd2, w.finished(1, 1))
                        pool.wait_ge(s_cent2, w.finished(1, 2))
                        nc.gpsimd.tensor_tensor(y_out[:], cent2[:],
                                                rstd2[:].rearrange("p (c o) -> p c o", o=1).to_broadcast([P, C, D]),
                                                ALU.mult).then_inc(s_out, 1)
                    if w.unit_before(slot) and slot - 1 != LAST:
                        pool.wait_ge(s_h_hi, w.carried(slot))
                        nc.gpsimd.tensor_tensor(h_lo[made][:], h[made][:], raw(h_hi[made][:]),
                                                ALU.subtract).then_inc(s_h_lo, 1)
                    if slot == 4 and w.prepares():
                        pool.wait_ge(s_h0_hi, w.prepared(1, 1))
                        nc.gpsimd.tensor_tensor(h_lo[0][:], h[0][:], raw(h_hi[0][:]),
                                                ALU.subtract).then_inc(s_h0_lo, 1)
                    if w.unit(slot):
                        pool.wait_ge(s_z, w.units(slot + 1))
                        nc.gpsimd.tensor_tensor(z_h[:], z_gate[:], h[layer][:], ALU.mult).then_inc(s_zh, 1)

            all_windows(window, pool)

        @block.scalar
        def _(act):
            act.dma_start(wih_t[:], wiht).then_inc(s_weights, 16)
            act.dma_start(wl_t[:], wlt.rearrange("l p d -> p l d")).then_inc(s_weights, 16)
            act.dma_start(whh_t[:], whht).then_inc(s_weights, 16)
            act.dma_start(bih_cols[:], bih).then_inc(s_small, 16)
            act.dma_start(bhh_cols[:], bhh).then_inc(s_small, 16)
            act.dma_start(mask_cols[:], mask).then_inc(s_small, 16)
            act.dma_start(bias0[:], b0.partition_broadcast(P)).then_inc(s_small, 16)

            def evacuate(dst, src):
                return nc.scalar.activation(dst, src, ACT.Copy)

            def weights():
                for l in range(LAYERS):
                    act.wait_ge(s_w_prod, l + 1)
                    evacuate(wc_hi[:, l, :], product_bank[l][:, 0:G * D]).then_inc(s_wc_hi, 1)

            def window(w):

                def adjt_hi_of(j):
                    evacuate(adjt_hi[:, j, :], adjt_in[:, j, :]).then_inc(s_adjt_hi, 1)

                def row_sum_of(c):
                    nc.scalar.activation(sum_of[:, c, :], adj_in[:, c, :], ACT.Copy,
                                         accum_out=row_sum[:, c:c + 1]).then_inc(s_row_sum, 1)

                def y_hi_of(half):
                    act.wait_ge(s_xw, w.prepared(2, half + 1))
                    evacuate(y_hi[:, 2 * half:2 * half + 2, 0:D],
                             ps_b[half][:].rearrange("p (c k d) -> p c k d", c=2, k=2)[:, :, 1, :]).then_inc(s_y_hi, 1)

                if w.prepares():
                    kept = act.snap(w.batch(-1) % KEPT)
                for slot in range(SLOTS):
                    made = UNITS[slot - 1][1] + 1
                    if w.prepares() and slot == 0:
                        act.wait_ge(s_xt_in, w.prepared(16, 16))
                        evacuate(xt_hi[:], xt_in[:]).then_inc(s_xt_hi, 1)
                    if w.unit_before(slot):
                        act.wait_ge(s_npre, w.units(slot))
                        nc.scalar.activation(n_gate[:], n_pre[:], ACT.Tanh,
                                             bias=bih_cols[:, 2:3]).then_inc(s_n, 1)
                    if w.unit(slot):
                        act.wait_ge(s_agg, w.units(slot + 1))
                        evacuate(agg_hi[:], ps_tok[:]).then_inc(s_agg_hi, 1)
                    if w.prepares():
                        if slot == 0:
                            act.wait_ge(s_adjt_in, w.prepared(16, 16))
                            adjt_hi_of(0)
                            adjt_hi_of(1)
                        if slot == 1:
                            act.wait_ge(s_adj_in, w.prepared(16, 16))
                            for c in range(C):
                                row_sum_of(c)
                        if slot == 4:
                            if w.unit(4):
                                act.wait_ge(s_agg, w.units(5))
                            act.wait_ge(s_x1, w.prepared(C, C))
                            evacuate(tok_hi[:], x1[:].rearrange("p c d -> p (c d)")).then_inc(s_x1_hi, 1)
                            evacuate(x1_kept[:, bass.ds(kept, 1), :, :].rearrange("p o c d -> p (o c d)"),
                                     x1[:].rearrange("p c d -> p (c d)")).then_inc(s_x1_kept, 1)
                    if w.first == -1 and slot == 2:
                        weights()
                    if slot < 4 and w.unit(slot + 1):
                        act.wait_ge(s_tok, w.turned(slot + 2))
                        evacuate(tok_hi[:], ps_tok[:]).then_inc(s_tok_hi, 1)
                    if w.unit_before(slot) and slot - 1 != LAST:
                        act.wait_ge(s_h, w.units(slot))
                        evacuate(h_hi[made][:], h[made][:]).then_inc(s_h_hi, 1)
                    if w.prepares() and slot == 0:
                        y_hi_of(0)
                        y_hi_of(1)
                    if w.prepares() and slot == 4:
                        act.wait_ge(s_x1t, w.prepared(1, 1))
                        evacuate(h[0][:], ps_b[1][:]).then_inc(s_h0, 1)
                    if w.prepares() and slot == 1:
                        act.wait_ge(s_nsum, w.prepared(1, 1))
                        evacuate(mean_t[:], ps_b[2][:]).then_inc(s_nsum_out, 1)
                    if w.unit(slot):
                        act.wait_ge(s_r_sum, w.units(slot + 1))
                        if w.first > 0 or slot > 0:
                            act.wait_ge(s_rhn, w.units(slot))
                        nc.scalar.activation(r_gate[:], ps_r[:], ACT.Sigmoid, bias=rz_bias[:, 0:1]).then_inc(s_r, 1)
                    if w.prepares() and slot == 4:
                        act.wait_ge(s_h0, w.prepared(1, 1))
                        evacuate(h_hi[0][:], h[0][:]).then_inc(s_h0_hi, 1)
                    if w.unit(slot):
                        act.wait_ge(s_z_sum, w.units(slot + 1))
                        if w.first > 0 or slot > 0:
                            act.wait_ge(s_h, w.units(slot))
                        nc.scalar.activation(z_gate[:], ps_z[:], ACT.Sigmoid, bias=rz_bias[:, 1:2]).then_inc(s_z, 1)
                    if w.prepares():
                        if slot == 0:
                            adjt_hi_of(2)
                            adjt_hi_of(3)

            all_windows(window, act)

        @block.vector
        def _(dve):
            def low_part(dst, src, hi):
                return nc.vector.tensor_tensor(dst, src, raw(hi), ALU.subtract)

            dve.wait_ge(s_w0, 16)
            nc.vector.tensor_copy(w0_hi[:], w0_in[:]).then_inc(s_w0, 1)
            dve.wait_ge(s_w0, 17)
            low_part(w0_lo[:], w0_in[:], w0_hi[:]).then_inc(s_w0, 1)
            dve.wait_ge(s_small, 4 * 16)

            def weights():
                nc.vector.tensor_tensor(rz_bias[:], bih_cols[:, 0:2], bhh_cols[:, 0:2], ALU.add).then_inc(s_whh, 1)
                dve.wait_ge(s_weights, 3 * 16)
                nc.vector.tensor_copy(whh_hi[:], whh_t[:]).then_inc(s_whh, 1)
                dve.wait_ge(s_whh, 2)
                low_part(whh_lo[:], whh_t[:], whh_hi[:]).then_inc(s_whh, 1)
                for l in range(LAYERS):
                    dve.wait_ge(s_wc_hi, l + 1)
                    low_part(wc_lo[:, l, :], product_bank[l][:, 0:G * D], wc_hi[:, l, :]).then_inc(s_wc_lo, 1)

            def window(w):
                prev = w.units

                def xw_parts(half):
                    ps = ps_b[half][:].rearrange("p (c k d) -> p c k d", c=2, k=2)
                    dve.wait_ge(s_y_hi, w.prepared(2, half + 1))
                    low_part(y_lo[:, 2 * half:2 * half + 2, 0:D], ps[:, :, 1, :], y_hi[:, 2 * half:2 * half + 2, 0:D])
                    nc.vector.tensor_tensor(own[:, 2 * half:2 * half + 2, :], ps[:, :, 0, :],
                                            bias0[:].rearrange("p (o d) -> p o d", o=1).to_broadcast([P, 2, D]),
                                            ALU.add).then_inc(s_own, 1)

                def mean_parts():
                    dve.wait_ge(s_nsum_tok, w.prepared(1, 1))
                    dve.wait_ge(s_rinv, w.prepared(2, 2))
                    for c in range(C):
                        last = nc.vector.scalar_tensor_tensor(
                            out=mixed[:, c, :], in0=ps_b[0][:, c * D:(c + 1) * D],
                            scalar=row_inv[:, c:c + 1], in1=own[:, c, :], op0=ALU.mult, op1=ALU.add)
                    last.then_inc(s_mixed, 1)

                def stats1_of(cs):
                    for c in cs:
                        nc.vector.bn_stats(stats1[:, c, :], pre1[:, c, :]).then_inc(s_stats1, 1)

                def edges_of(cs):
                    for c in cs:
                        nc.vector.tensor_scalar(edges[:, bass.ds(ring, 1), c, :].rearrange("p o m -> p (o m)"),
                                                adj_in[:, c, :], 0.0, None, ALU.not_equal).then_inc(s_edges, 1)

                if w.prepares():
                    ring = dve.snap(w.batch(-1) % RING)
                if w.finishes():
                    kept = dve.snap(w.batch(3) % KEPT)

                for slot in range(SLOTS):
                    made = UNITS[slot - 1][1] + 1
                    if w.unit_before(slot):
                        dve.wait_ge(s_in_sum, w.units(slot))
                        dve.wait_ge(s_rhn, w.units(slot))
                        nc.vector.tensor_tensor(n_pre[:], ps_in[:], r_hn[:], ALU.add).then_inc(s_npre, 1)
                    if w.prepares():
                        if slot == 0:
                            dve.wait_ge(s_xt_hi, w.prepared(1, 1))
                            low_part(xt_lo[:], xt_in[:], xt_hi[:]).then_inc(s_xt_lo, 1)
                        if slot == 1:
                            xw_parts(1)
                        if slot == 3:
                            dve.wait_ge(s_x_in, w.prepared(16, 16))
                            dve.wait_ge(s_mixed, w.prepared(1, 1))
                            nc.vector.scalar_tensor_tensor(out=pre1[:], in0=mixed[:], scalar=0.0, in1=x_in[:],
                                                           op0=ALU.max, op1=ALU.add).then_inc(s_pre1, 1)
                            dve.wait_ge(s_pre1, w.prepared(1, 1))
                            stats1_of((0, 1))
                        if slot == 4:
                            dve.wait_ge(s_rstd1, w.prepared(1, 1))
                            for c in range(C):
                                nc.vector.tensor_scalar(x1[:, c, :], pre1[:, c, :], mv1[:, c, 0:1],
                                                        rstd1[:, c:c + 1], ALU.subtract, ALU.mult).then_inc(s_x1, 1)
                    if w.unit_before(slot):
                        dve.wait_ge(s_n, w.units(slot))
                        nc.vector.scalar_tensor_tensor(out=zm1_n[:], in0=z_gate[:], scalar=1.0, in1=n_gate[:],
                                                       op0=ALU.subtract, op1=ALU.mult).then_inc(s_zm1n, 1)
                    if w.unit(slot):
                        dve.wait_ge(s_agg_hi, w.units(slot + 1))
                        low_part(agg_lo[:], ps_tok[:], agg_hi[:]).then_inc(s_agg_lo, 1)
                    if w.first == -1 and slot == 2:
                        weights()
                    if w.prepares() and slot == 3:
                        stats1_of((2, 3))
                        dve.wait_ge(s_stats1, w.prepared(C, C))
                    if w.unit_before(slot):
                        dve.wait_ge(s_zh, w.units(slot))
                        dve.wait_ge(s_zm1n, w.units(slot))
                        nc.vector.tensor_tensor(h[made][:], z_h[:], zm1_n[:], ALU.subtract).then_inc(s_h, 1)
                    if w.prepares():
                        if slot == 2:
                            mean_parts()
                        if slot == 3:
                            for c in range(C):
                                nc.vector.bn_aggr(mv1[:, c, :], stats1[:, c, :]).then_inc(s_mv1, 1)
                            dve.wait_ge(s_mv1, w.prepared(C, C))
                            nc.vector.tensor_scalar(var1[:], mv1[:, :, 1], LN_EPS, None, ALU.add).then_inc(s_var1, 1)
                        if slot == 4:
                            if w.unit(LAST):
                                dve.wait_ge(s_agg, w.units(LAST + 1))
                            edges_of(range(C))
                    if slot == 1 and w.finishes():
                        dve.wait_ge(s_last, w.finished(1, 1))
                        dve.wait_ge(s_x1_kept, w.finished(1, 1))
                        dve.wait_ge(s_cent2, w.freed())
                        b = w.batch(3)
                        for c in range(C):
                            last = nc.vector.scalar_tensor_tensor(
                                out=pre2[:, c, :], in0=ps_b[1][:, c * P:(c + 1) * P],
                                scalar=mask_cols[:, bass.ds(b * C + c, 1)],
                                in1=x1_kept[:, bass.ds(kept, 1), c, :].rearrange("p o d -> p (o d)"),
                                op0=ALU.mult, op1=ALU.add)
                        last.then_inc(s_end_read, 1)
                        dve.wait_ge(s_end_read, w.finished(1, 1))
                        for c in range(C):
                            nc.vector.bn_stats(stats2[:, c, :], pre2[:, c, :]).then_inc(s_stats2, 1)
                        dve.wait_ge(s_stats2, w.finished(C, C))
                    if w.prepares() and slot == 1:
                        dve.wait_ge(s_row_sum, w.prepared(C, C))
                        nc.vector.tensor_scalar(row_eps[:], row_sum[:], ROW_EPS, None, ALU.add).then_inc(s_rinv, 1)
                    if slot == 1 and w.finishes():
                        for c in range(C):
                            nc.vector.bn_aggr(mv2[:, c, :], stats2[:, c, :]).then_inc(s_mv2, 1)
                        dve.wait_ge(s_mv2, w.finished(C, C))
                        nc.vector.tensor_scalar(var2[:], mv2[:, :, 1], LN_EPS, None, ALU.add).then_inc(s_var2, 1)
                    if slot < 4 and w.unit(slot + 1):
                        dve.wait_ge(s_tok_hi, w.turned(slot + 2))
                        low_part(tok_lo[:], ps_tok[:], tok_hi[:]).then_inc(s_tok_lo, 1)
                    if w.prepares():
                        if slot == 0:
                            xw_parts(0)
                        if slot == 1:
                            dve.wait_ge(s_rinv, w.prepared(2, 1))
                            nc.vector.reciprocal(row_inv[:], row_eps[:]).then_inc(s_rinv, 1)
                    if w.unit(slot):
                        dve.wait_ge(s_r, w.units(slot + 1))
                        nc.vector.scalar_tensor_tensor(out=r_hn[:], in0=ps_hn[:], scalar=bhh_cols[:, 2:3],
                                                       in1=r_gate[:], op0=ALU.add, op1=ALU.mult).then_inc(s_rhn, 1)

            all_windows(window, dve)

        @block.tensor
        def _(pe):
            def turn(dst, src):
                return nc.tensor.transpose(dst, src, ident[:])

            def split_product(dst, lhs_hi, lhs_lo, rhs_hi, rhs_lo, start, stop):
                nc.tensor.matmul(dst, lhs_hi, rhs_hi, start=start, stop=False)
                nc.tensor.matmul(dst, lhs_hi, rhs_lo, start=False, stop=False)
                return nc.tensor.matmul(dst, lhs_lo, rhs_hi, start=False, stop=stop)

            def weights():
                pe.wait_ge(s_weights, 3 * 16)
                for l in range(LAYERS):
                    nc.tensor.matmul(product_bank[l][:, 0:G * D], wl_t[:, l, :], wih_t[:],
                                     start=True, stop=True).then_inc(s_w_prod, 1)

            pe.wait_ge(s_const, 3)
            pe.wait_ge(s_w0, 18)

            def window(w):

                def own_products(half):
                    for c in range(2):
                        ts = slice((2 * half + c) * P, (2 * half + c + 1) * P)
                        last = split_product(ps_b[half][:, c * 2 * D:(c + 1) * 2 * D], xt_hi[:, ts], xt_lo[:, ts],
                                             w0_hi[:], w0_lo[:], True, True)
                    last.then_inc(s_xw, 1)

                def neighbour_sums(js):
                    for j in js:
                        pe.wait_ge(s_adjt_lo, w.prepared(C, j + 1))
                        last = split_product(ps_b[2][:], y_hi[:, j, :], y_lo[:, j, :], adjt_hi[:, j, :],
                                             adjt_lo[:, j, :], j == 0, j == C - 1)
                    return last

                def gate(dst, g, hi, lo, weights_hi, weights_lo, start, stop):
                    gs = slice(g * D, (g + 1) * D)
                    return split_product(dst[:], weights_hi[:, gs], weights_lo[:, gs], hi[:], lo[:], start, stop)

                ring = [pe.snap(w.batch(back) % RING) if w.first - back >= 0 else None for back in range(RING)]
                for slot in range(SLOTS):
                    unit = w.unit(slot)
                    layer = UNITS[slot][1]
                    if unit:
                        if slot == 0:
                            if w.first == 0:
                                pe.wait_ge(s_wc_lo, LAYERS)
                            pe.wait_ge(s_x1_lo, w.young(1, 1))
                            pe.wait_ge(s_edges, w.young(C, C))
                        else:
                            pe.wait_ge(s_tok_lo, w.turned(slot + 1))
                        for c in range(C):
                            ts = slice(c * P, (c + 1) * P)
                            from_c = edges[:, bass.ds(ring[UNITS[slot][0]], 1), c, :].rearrange("p o m -> p (o m)")
                            nc.tensor.matmul(ps_tok[:], tok_hi[:, ts], from_c, start=c == 0, stop=False)
                            last = nc.tensor.matmul(ps_tok[:], tok_lo[:, ts], from_c, start=False, stop=c == C - 1)
                        last.then_inc(s_agg, 1)
                    if w.first == -1 and slot == 2:
                        weights()
                    if w.prepares():
                        if slot == 1:
                            pe.wait_ge(s_own, w.prepared(2, 1))
                            if w.first >= 0:
                                pe.wait_ge(s_nsum_out, w.prepared(1, 0))
                            neighbour_sums((0, 1))
                        if slot == 2:
                            pe.wait_ge(s_nsum_out, w.prepared(1, 1))
                            for c in range(C):
                                last = turn(ps_b[0][:, c * P:(c + 1) * P], mean_t[:, c * P:(c + 1) * P])
                            last.then_inc(s_nsum_tok, 1)
                    if slot == 1 and w.finishes():
                        if w.prepares():
                            pe.wait_ge(s_own, w.prepared(2, 2))
                        pe.wait_ge(s_h, w.last_layers())
                        for c in range(C):
                            last = turn(ps_b[1][:, c * P:(c + 1) * P], h[LAYERS][:, c * P:(c + 1) * P])
                        last.then_inc(s_last, 1)
                    if unit:
                        if slot == 0:
                            if w.first == 0:
                                pe.wait_ge(s_wc_lo, LAYERS)
                                pe.wait_ge(s_whh, 3)
                            pe.wait_ge(s_h0_lo, w.young(1, 1))
                        else:
                            pe.wait_ge(s_h_lo, w.until_made(slot, w.carried))
                        started = w.first > 0 or slot > 0
                        if started:
                            pe.wait_ge(s_rhn, w.units(slot))
                        gate(ps_hn, 2, h_hi[layer], h_lo[layer], whh_hi, whh_lo, True, True)
                        if started:
                            pe.wait_ge(s_z, w.units(slot))
                        gate(ps_r, 0, h_hi[layer], h_lo[layer], whh_hi, whh_lo, True, False)
                        gate(ps_z, 1, h_hi[layer], h_lo[layer], whh_hi, whh_lo, True, False)
                    if w.prepares() and slot == 4:
                        pe.wait_ge(s_x1, w.prepared(C, C))
                        if w.finishes():
                            pe.wait_ge(s_end_read, w.finished(1, 1))
                        for c in range(C):
                            last = turn(ps_b[1][:, c * P:(c + 1) * P], x1[:, c, :])
                        last.then_inc(s_x1t, 1)
                    if unit:
                        pe.wait_ge(s_agg_lo, w.units(slot + 1))
                    if slot < 4 and w.unit(slot + 1):
                        t = UNITS[slot + 1][1]
                        pe.wait_ge(s_h, w.until_made(slot + 1, w.units))
                        for c in range(C):
                            last = turn(ps_tok[:, c * P:(c + 1) * P], h[t][:, c * P:(c + 1) * P])
                        last.then_inc(s_tok, 1)
                    if w.prepares():
                        if slot == 0:
                            pe.wait_ge(s_xt_lo, w.prepared(1, 1))
                            if w.first >= 0:
                                pe.wait_ge(s_mixed, w.prepared(1, 0))
                                pe.wait_ge(s_h0, w.prepared(1, 0))
                            own_products(0)
                            own_products(1)
                        if slot == 1:
                            pe.wait_ge(s_own, w.prepared(2, 2))
                            neighbour_sums((2, 3)).then_inc(s_nsum, 1)
                    if unit:
                        wi_hi, wi_lo = wc_hi[:, layer, :], wc_lo[:, layer, :]
                        gate(ps_r, 0, agg_hi, agg_lo, wi_hi, wi_lo, False, True).then_inc(s_r_sum, 1)
                        gate(ps_z, 1, agg_hi, agg_lo, wi_hi, wi_lo, False, True).then_inc(s_z_sum, 1)
                        if started:
                            pe.wait_ge(s_npre, w.units(slot))
                        gate(ps_in, 2, agg_hi, agg_lo, wi_hi, wi_lo, True, True).then_inc(s_in_sum, 1)

            all_windows(window, pe)


def kernel(x, adj, nodemask, L0_gnn_weight, L0_gnn_bias, L1_gnn_weight, L1_gnn_w_ih, L1_gnn_w_hh, L1_gnn_b_ih,
           L1_gnn_b_hh):
    import numpy as _np
    import concourse.bacc as _bacc
    from concourse import mybir as _mybir
    from concourse.bass_utils import run_bass_kernel_spmd as _run

    x, adj, nodemask = _np.asarray(x), _np.asarray(adj), _np.asarray(nodemask)
    batches, nodes = nodemask.shape
    laid_out = {
        "x": x,
        "x_t": x.transpose(0, 2, 1),
        "adj": adj,
        "adj_t": adj.transpose(0, 2, 1),
        "mask": nodemask.reshape(batches * nodes // P, P).transpose(1, 0),
        "w0": _np.asarray(L0_gnn_weight),
        "b0": _np.asarray(L0_gnn_bias),
        "wl_t": _np.asarray(L1_gnn_weight).transpose(0, 2, 1),
        "w_ih_t": _np.asarray(L1_gnn_w_ih).transpose(1, 0),
        "w_hh_t": _np.asarray(L1_gnn_w_hh).transpose(1, 0),
        "b_ih": _np.asarray(L1_gnn_b_ih).reshape(3, P).transpose(1, 0),
        "b_hh": _np.asarray(L1_gnn_b_hh).reshape(3, P).transpose(1, 0),
    }
    nc = _bacc.Bacc("TRN2", target_bir_lowering=False, num_devices=1)
    arrays, args = {}, []
    for name, a in laid_out.items():
        a = _np.ascontiguousarray(a)
        arrays[f"in_{name}_dram"] = a
        args.append(nc.dram_tensor(f"in_{name}_dram", a.shape, _mybir.dt.from_np(a.dtype), kind="ExternalInput").ap())
    args.append(nc.dram_tensor("out_dram", x.shape, _mybir.dt.float32, kind="ExternalOutput").ap())
    program(nc, *args)
    return _run(nc, [arrays], core_ids=[0]).results[0]["out_dram"]
```

```python
from contextlib import ExitStack

import concourse.bass as bass
from concourse import mybir

ALU = mybir.AluOpType
ACT = mybir.ActivationFunctionType
F32 = mybir.dt.float32
F32R = mybir.dt.float32r

P = 128
LAYERS = 5
LN_EPS = 1e-5
ROW_EPS = 1e-8

UNITS = ((0, 0), (1, 2), (2, 4), (0, 1), (1, 3))
SLOTS = len(UNITS)
LAST = UNITS.index((2, LAYERS - 1))
FIRST_WINDOWS = (((0, 0), None, (0, 1), None, None),
                 ((0, 0), (1, 2), (0, 1), (1, 3), None))
LAST_WINDOWS = (((0, 0), (1, 2), (0, 1), (2, 4), (1, 3)),
                (None, (1, 2), (2, 4), (1, 3), None))


def units_of(batches, n):
    if 0 <= n < 2:
        return FIRST_WINDOWS[n]
    if batches - 1 <= n < batches + 1:
        return LAST_WINDOWS[n - batches + 1]
    return tuple(u if 0 <= n - u[0] < batches else None for u in UNITS)


def place(batches, batch, layer):
    for n in range(batch, batch + 3):
        if (n - batch, layer) in units_of(batches, n):
            return n, units_of(batches, n).index((n - batch, layer))


def count(batches, n, slot, layers):
    return sum(
        unit is not None and unit[1] in layers
        for m in range(0, n + 1)
        for s, unit in enumerate(units_of(batches, m))
        if m < n or s < slot
    )


class Window:

    def __init__(self, batches, first, trip=None):
        self.batches, self.first, self.trip = batches, first, trip

    def value(self, of_number):
        start = of_number(self.first)
        if self.trip is None:
            return start
        return self.trip * (of_number(self.first + 1) - start) + start

    def batch(self, back):
        return self.value(lambda n: n - back)

    def unit(self, slot):
        return units_of(self.batches, self.first)[slot]

    def unit_before(self, slot):
        if slot == 0:
            return units_of(self.batches, self.first - 1)[SLOTS - 1]
        return self.unit(slot - 1)

    def prepares(self):
        return -1 <= self.first < self.batches - 1

    def finishes(self):
        return 3 <= self.first < self.batches + 3

    def ramps(self):
        return self.first < 2

    def state_slot(self):
        return 3 if self.ramps() else 4

    def loads(self):
        return -1 <= self.first < self.batches - 2

    def units(self, slot, layers=range(LAYERS)):
        return self.value(lambda n: count(self.batches, n, slot, layers))

    def carried(self, slot):
        return self.units(slot, range(LAYERS - 1))

    def turned(self, slot):
        return self.units(slot, range(1, LAYERS))

    def until_made(self, slot, layers=range(LAYERS)):
        def up_to(n):
            back, layer = units_of(self.batches, n)[slot]
            m, s = place(self.batches, n - back, layer - 1)
            return count(self.batches, m, s + 1, layers)
        return self.value(up_to)

    def prepared(self, each, k):
        return self.value(lambda n: each * (n + 1) + k)

    def young(self, each, k):
        return self.value(lambda n: each * n + k)

    def finished(self, each, k):
        return self.value(lambda n: each * (n - 3) + k)

    def freed(self, each=1):
        return self.value(lambda n: each * (n - 2))

    def last_layers(self):
        def up_to(n):
            m, s = place(self.batches, n - 3, LAYERS - 1)
            return count(self.batches, m, s + 1, range(LAYERS))
        return self.value(up_to)


def program(nc, x, xt, adj, adjt, mask, w0, b0, wlt, wiht, whht, gru_b, out):
    B, N, D = x.shape
    C = N // P
    G = 3
    assert D == P and N == 512 and wlt.shape[0] == LAYERS and B >= 6

    with ExitStack() as ctx:
        def sb(name, shape, dtype=F32):
            return ctx.enter_context(nc.sbuf_tensor(name, shape, dtype))

        def bank(name):
            return ctx.enter_context(nc.psum_tensor(name, [P, 512], F32))

        def sem(name):
            return ctx.enter_context(nc.semaphore(name))

        ident = sb("ident", [P, P])
        zero_tile = sb("zero_tile", [P, P])
        minus_half = sb("minus_half", [P, C])
        first_sigmoid = sb("first_sigmoid", [P, C])
        mask_cols = sb("mask_cols", [P, B * C])
        bias0 = sb("bias0", [P, D])
        gru_bias = sb("gru_bias", [P, 2 * G])
        bih_cols, bhh_cols = gru_bias[:, 0:G], gru_bias[:, G:2 * G]
        rz_bias = sb("rz_bias", [P, 2])
        w0_in = sb("w0_in", [P, 2 * D])
        w0_hi = sb("w0_hi", [P, 2 * D], F32R)
        w0_lo = sb("w0_lo", [P, 2 * D], F32R)
        wih_t = sb("wih_t", [P, G * D])
        whh_t = sb("whh_t", [P, G * D])
        wl_t = sb("wl_t", [P, LAYERS, D])
        whh_hi = sb("whh_hi", [P, G * D], F32R)
        whh_lo = sb("whh_lo", [P, G * D], F32R)
        wc_hi = sb("wc_hi", [P, LAYERS, G * D], F32R)
        wc_lo = sb("wc_lo", [P, LAYERS, G * D], F32R)

        adj_in = sb("adj_in", [P, C, N])
        adjt_in = sb("adjt_in", [P, C, N])
        xt_in = sb("xt_in", [P, N])
        x_in = sb("x_in", [P, C, D])
        RING, KEPT = 3, 4
        edges = sb("edges", [P, RING, C, N], F32R)
        x1_kept = sb("x1_kept", [P, KEPT, C, D])
        h = [sb(f"h{i}", [P, N]) for i in range(LAYERS + 1)]
        h_hi = [sb(f"h_hi{i}", [P, N], F32R) for i in range(LAYERS)]
        h_lo = [sb(f"h_lo{i}", [P, N], F32R) for i in range(LAYERS)]

        adjt_hi = sb("adjt_hi", [P, C, N], F32R)
        adjt_lo = sb("adjt_lo", [P, C, N], F32R)
        xt_hi = sb("xt_hi", [P, N], F32R)
        xt_lo = sb("xt_lo", [P, N], F32R)
        y_hi = sb("y_hi", [P, C, D], F32R)
        y_lo = sb("y_lo", [P, C, D], F32R)
        own = sb("own", [P, C, D])
        sum_of = sb("sum_of", [P, C, N])
        mean_t = sb("mean_t", [P, N])
        row_sum = sb("row_sum", [P, C])
        row_eps = sb("row_eps", [P, C])
        row_inv = sb("row_inv", [P, C])
        mixed = sb("mixed", [P, C, D])
        pre1 = sb("pre1", [P, C, D])
        stats1 = sb("stats1", [P, C, 6])
        mv1 = sb("mv1", [P, C, 2])
        var1 = sb("var1", [P, C])
        rstd1 = sb("rstd1", [P, C])
        x1 = sb("x1", [P, C, D])

        tok_hi = sb("tok_hi", [P, N], F32R)
        tok_lo = sb("tok_lo", [P, N], F32R)
        agg_hi = sb("agg_hi", [P, N], F32R)
        agg_lo = sb("agg_lo", [P, N], F32R)
        r_gate = sb("r_gate", [P, N])
        z_gate = sb("z_gate", [P, N])
        r_hn = sb("r_hn", [P, N])
        n_pre = sb("n_pre", [P, N])
        n_gate = sb("n_gate", [P, N])
        z_h = sb("z_h", [P, N])
        zm1_n = sb("zm1_n", [P, N])

        pre2 = sb("pre2", [P, C, D])
        stats2 = sb("stats2", [P, C, 6])
        mv2 = sb("mv2", [P, C, 2])
        var2 = sb("var2", [P, C])
        rstd2 = sb("rstd2", [P, C])
        cent2 = sb("cent2", [P, C, D])
        y_out = sb("y_out", [P, C, D])

        ps_tok = bank("ps_tok")
        ps_hn, ps_r, ps_z, ps_in = bank("ps_hn"), bank("ps_r"), bank("ps_z"), bank("ps_in")
        ps_b = [bank(f"ps_b{i}") for i in range(3)]

        s_small = sem("s_small")
        s_bias0 = sem("s_bias0")
        s_weights = sem("s_weights")
        s_adj_in = sem("s_adj_in")
        s_adjt_in = sem("s_adjt_in")
        s_x_in = sem("s_x_in")
        s_xt_in = sem("s_xt_in")
        s_stored = sem("s_stored")
        s_const = sem("s_const")
        s_w0 = sem("s_w0")
        s_whh = sem("s_whh")
        s_w_prod = sem("s_w_prod")
        s_wc_hi = sem("s_wc_hi")
        s_wc_lo = sem("s_wc_lo")
        s_xt_hi = sem("s_xt_hi")
        s_xt_lo = sem("s_xt_lo")
        s_adjt_hi = sem("s_adjt_hi")
        s_adjt_lo = sem("s_adjt_lo")
        s_row_sum = sem("s_row_sum")
        s_rinv = sem("s_rinv")
        s_xw = sem("s_xw")
        s_y_hi = sem("s_y_hi")
        s_own = sem("s_own")
        s_nsum = sem("s_nsum")
        s_nsum_out = sem("s_nsum_out")
        s_nsum_tok = sem("s_nsum_tok")
        s_mixed = sem("s_mixed")
        s_pre1 = sem("s_pre1")
        s_stats1 = sem("s_stats1")
        s_mv1 = sem("s_mv1")
        s_var1 = sem("s_var1")
        s_rstd1 = sem("s_rstd1")
        s_x1 = sem("s_x1")
        s_x1_kept = sem("s_x1_kept")
        s_x1_hi = sem("s_x1_hi")
        s_x1_lo = sem("s_x1_lo")
        s_x1t = sem("s_x1t")
        s_h0 = sem("s_h0")
        s_h0_hi = sem("s_h0_hi")
        s_h0_lo = sem("s_h0_lo")
        s_edges = sem("s_edges")
        s_tok = sem("s_tok")
        s_tok_hi = sem("s_tok_hi")
        s_tok_lo = sem("s_tok_lo")
        s_agg = sem("s_agg")
        s_agg_hi = sem("s_agg_hi")
        s_agg_lo = sem("s_agg_lo")
        s_r_sum = sem("s_r_sum")
        s_z_sum = sem("s_z_sum")
        s_in_sum = sem("s_in_sum")
        s_r = sem("s_r")
        s_z = sem("s_z")
        s_rhn = sem("s_rhn")
        s_npre = sem("s_npre")
        s_n = sem("s_n")
        s_zh = sem("s_zh")
        s_zm1n = sem("s_zm1n")
        s_h = sem("s_h")
        s_h_hi = sem("s_h_hi")
        s_h_lo = sem("s_h_lo")
        s_last = sem("s_last")
        s_end_read = sem("s_end_read")
        s_stats2 = sem("s_stats2")
        s_mv2 = sem("s_mv2")
        s_var2 = sem("s_var2")
        s_rstd2 = sem("s_rstd2")
        s_cent2 = sem("s_cent2")
        s_out = sem("s_out")

        def raw(ap):
            return ap.bitcast(F32)

        def all_windows(window, eng):
            for n in range(-1, 3):
                window(Window(B, n))
            with eng.Fori(0, B - 4) as trip:
                window(Window(B, 3, trip))
            for n in range(B - 1, B + 3):
                window(Window(B, n))

        product_bank = (ps_hn, ps_in, ps_tok, ps_r, ps_z)

        block = ctx.enter_context(nc.Block())

        @block.sync
        def _(sp):
            def load_xt(b):
                sp.dma_start(xt_in[:], xt[b]).then_inc(s_xt_in, 16)

            def load_adjt(b):
                sp.dma_start(adjt_in[:], adjt[b].rearrange("(c p) m -> p c m", p=P)).then_inc(s_adjt_in, 16)

            def load_x(b):
                sp.dma_start(x_in[:], x[b].rearrange("(c p) d -> p c d", p=P)).then_inc(s_x_in, 16)

            def load_adj(b):
                sp.dma_start(adj_in[:], adj[b].rearrange("(c p) m -> p c m", p=P)).then_inc(s_adj_in, 16)

            sp.sem_inc(s_stored, 16)
            load_xt(0)
            sp.dma_start(w0_in[:].rearrange("p (k d) -> p k d", k=2),
                         w0.rearrange("(k p) d -> p k d", p=P)).then_inc(s_w0, 16)
            load_adjt(0)
            load_adj(0)
            load_x(0)

            def window(w):
                if w.loads():
                    b = w.batch(-2)
                    sp.wait_ge(s_xt_lo, w.prepared(1, 1))
                    load_xt(b)
                    sp.wait_ge(s_adjt_lo, w.prepared(C, C))
                    load_adjt(b)
                if w.finishes():
                    sp.wait_ge(s_out, w.finished(1, 1))
                    sp.dma_start(out[w.batch(3)].rearrange("(c p) d -> p c d", p=P), y_out[:]).then_inc(s_stored, 16)
                if w.loads():
                    b = w.batch(-2)
                    sp.wait_ge(s_pre1, w.prepared(1, 1))
                    load_x(b)
                    sp.wait_ge(s_row_sum, w.prepared(C, C))
                    sp.wait_ge(s_edges, w.prepared(C, C))
                    load_adj(b)

            for n in range(-1, 3):
                window(Window(B, n))
            with sp.Fori(0, B - 5) as trip:
                window(Window(B, 3, trip))
            for n in range(B - 2, B + 3):
                window(Window(B, n))
            sp.wait_ge(s_stored, 16 * (B + 1))

        @block.gpsimd
        def _(pool):
            pool.sem_inc(s_cent2, 1)
            nc.gpsimd.memset(zero_tile[:], 0.0).then_inc(s_const, 1)
            nc.gpsimd.memset(minus_half[:], -0.5).then_inc(s_const, 1)
            pool.wait_ge(s_const, 2)
            nc.gpsimd.affine_select(out=ident[:], in_=zero_tile[:], compare_op=ALU.not_equal, fill=1.0, base=0,
                                    pattern=[[-1, P]], channel_multiplier=1).then_inc(s_const, 1)
            pool.dma_start(bias0[:], b0.partition_broadcast(P)).then_inc(s_bias0, 16)
            pool.dma_start(gru_bias[:], gru_b).then_inc(s_small, 16)
            pool.dma_start(mask_cols[:], mask).then_inc(s_small, 16)

            def window(w):

                def adjt_lo_of(j):
                    pool.wait_ge(s_adjt_hi, w.prepared(C, j + 1))
                    nc.gpsimd.tensor_tensor(adjt_lo[:, j, :], adjt_in[:, j, :], raw(adjt_hi[:, j, :]),
                                            ALU.subtract).then_inc(s_adjt_lo, 1)

                for slot in range(SLOTS):
                    made = w.unit_before(slot)[1] + 1 if w.unit_before(slot) else None
                    layer = w.unit(slot)[1] if w.unit(slot) else None
                    if w.prepares():
                        if slot == 0:
                            adjt_lo_of(0)
                            adjt_lo_of(1)
                        if slot == 1:
                            adjt_lo_of(2)
                            adjt_lo_of(3)
                        if slot == w.state_slot():
                            pool.wait_ge(s_x1_hi, w.prepared(1, 1))
                            nc.gpsimd.tensor_tensor(tok_lo[:], x1[:].rearrange("p c d -> p (c d)"),
                                                    raw(tok_hi[:]), ALU.subtract).then_inc(s_x1_lo, 1)
                    if w.prepares() and slot == w.state_slot() - 1:
                        pool.wait_ge(s_var1, w.prepared(1, 1))
                        nc.gpsimd.tensor_tensor(rstd1[:], var1[:], minus_half[:], ALU.pow).then_inc(s_rstd1, 1)
                    if slot == 2 and w.finishes():
                        pool.wait_ge(s_stored, w.freed(16))
                        pool.wait_ge(s_var2, w.finished(1, 1))
                        nc.gpsimd.tensor_tensor(rstd2[:], var2[:], minus_half[:], ALU.pow).then_inc(s_rstd2, 1)
                        nc.gpsimd.tensor_tensor(cent2[:], pre2[:], mv2[:, :, 0:1].to_broadcast([P, C, D]),
                                                ALU.subtract).then_inc(s_cent2, 1)
                        pool.wait_ge(s_rstd2, w.finished(1, 1))
                        pool.wait_ge(s_cent2, w.finished(1, 2))
                        nc.gpsimd.tensor_tensor(y_out[:], cent2[:],
                                                rstd2[:].rearrange("p (c o) -> p c o", o=1).to_broadcast([P, C, D]),
                                                ALU.mult).then_inc(s_out, 1)
                    if w.unit_before(slot) and made < LAYERS:
                        pool.wait_ge(s_h_hi, w.carried(slot))
                        nc.gpsimd.tensor_tensor(h_lo[made][:], h[made][:], raw(h_hi[made][:]),
                                                ALU.subtract).then_inc(s_h_lo, 1)
                    if slot == w.state_slot() and w.prepares():
                        pool.wait_ge(s_h0_hi, w.prepared(1, 1))
                        nc.gpsimd.tensor_tensor(h_lo[0][:], h[0][:], raw(h_hi[0][:]),
                                                ALU.subtract).then_inc(s_h0_lo, 1)
                    if w.unit(slot):
                        pool.wait_ge(s_z, w.units(slot + 1))
                        nc.gpsimd.tensor_tensor(z_h[:], z_gate[:], h[layer][:], ALU.mult).then_inc(s_zh, 1)

            all_windows(window, pool)

        @block.scalar
        def _(act):
            act.wait_ge(s_const, 2)
            nc.scalar.activation(first_sigmoid[:], minus_half[:], ACT.Sigmoid)
            act.dma_start(wih_t[:], wiht).then_inc(s_weights, 16)
            act.dma_start(wl_t[:], wlt.rearrange("l p d -> p l d")).then_inc(s_weights, 16)
            act.dma_start(whh_t[:], whht).then_inc(s_weights, 16)

            def evacuate(dst, src):
                return nc.scalar.activation(dst, src, ACT.Copy)

            def weights():
                for l in range(LAYERS):
                    act.wait_ge(s_w_prod, l + 1)
                    evacuate(wc_hi[:, l, :], product_bank[l][:, 0:G * D]).then_inc(s_wc_hi, 1)

            def window(w):

                def adjt_hi_of(j):
                    evacuate(adjt_hi[:, j, :], adjt_in[:, j, :]).then_inc(s_adjt_hi, 1)

                def row_sum_of(c):
                    nc.scalar.activation(sum_of[:, c, :], adj_in[:, c, :], ACT.Copy,
                                         accum_out=row_sum[:, c:c + 1]).then_inc(s_row_sum, 1)

                def y_hi_of(half):
                    act.wait_ge(s_xw, w.prepared(2, half + 1))
                    evacuate(y_hi[:, 2 * half:2 * half + 2, 0:D],
                             ps_b[half][:].rearrange("p (c k d) -> p c k d", c=2, k=2)[:, :, 1, :]).then_inc(s_y_hi, 1)

                if w.prepares():
                    kept = act.snap(w.batch(-1) % KEPT)
                for slot in range(SLOTS):
                    made = w.unit_before(slot)[1] + 1 if w.unit_before(slot) else None
                    if w.prepares() and slot == 0:
                        act.wait_ge(s_xt_in, w.prepared(16, 16))
                        evacuate(xt_hi[:], xt_in[:]).then_inc(s_xt_hi, 1)
                    if w.unit_before(slot):
                        act.wait_ge(s_npre, w.units(slot))
                        nc.scalar.activation(n_gate[:], n_pre[:], ACT.Tanh,
                                             bias=bih_cols[:, 2:3]).then_inc(s_n, 1)
                    if w.unit(slot):
                        act.wait_ge(s_agg, w.units(slot + 1))
                        evacuate(agg_hi[:], ps_tok[:]).then_inc(s_agg_hi, 1)
                    if w.prepares():
                        if slot == 0:
                            act.wait_ge(s_adjt_in, w.prepared(16, 16))
                            adjt_hi_of(0)
                            adjt_hi_of(1)
                            if w.first == -1:
                                adjt_hi_of(2)
                                adjt_hi_of(3)
                        if slot == 1:
                            act.wait_ge(s_adj_in, w.prepared(16, 16))
                            for c in range(C):
                                row_sum_of(c)
                        if slot == w.state_slot():
                            if w.first >= 0:
                                act.wait_ge(s_agg, w.units(slot + 1))
                            act.wait_ge(s_x1, w.prepared(C, C))
                            evacuate(tok_hi[:], x1[:].rearrange("p c d -> p (c d)")).then_inc(s_x1_hi, 1)
                            evacuate(x1_kept[:, bass.ds(kept, 1), :, :].rearrange("p o c d -> p (o c d)"),
                                     x1[:].rearrange("p c d -> p (c d)")).then_inc(s_x1_kept, 1)
                    if slot < 4 and w.unit(slot + 1):
                        act.wait_ge(s_tok, w.turned(slot + 2))
                        evacuate(tok_hi[:], ps_tok[:]).then_inc(s_tok_hi, 1)
                    if w.unit_before(slot) and made < LAYERS:
                        act.wait_ge(s_h, w.units(slot))
                        evacuate(h_hi[made][:], h[made][:]).then_inc(s_h_hi, 1)
                    if w.prepares() and slot == 0:
                        y_hi_of(0)
                        y_hi_of(1)
                    if w.first == -1 and slot == 0:
                        weights()
                    if w.prepares() and slot == w.state_slot():
                        act.wait_ge(s_x1t, w.prepared(1, 1))
                        evacuate(h[0][:], ps_b[1][:]).then_inc(s_h0, 1)
                    if w.prepares() and slot == 1:
                        act.wait_ge(s_nsum, w.prepared(1, 1))
                        evacuate(mean_t[:], ps_b[2][:]).then_inc(s_nsum_out, 1)
                    if w.unit(slot):
                        act.wait_ge(s_r_sum, w.units(slot + 1))
                        if w.first > 0 or slot > 0:
                            act.wait_ge(s_rhn, w.units(slot))
                        nc.scalar.activation(r_gate[:], ps_r[:], ACT.Sigmoid, bias=rz_bias[:, 0:1]).then_inc(s_r, 1)
                    if w.prepares() and slot == w.state_slot():
                        act.wait_ge(s_h0, w.prepared(1, 1))
                        evacuate(h_hi[0][:], h[0][:]).then_inc(s_h0_hi, 1)
                    if w.unit(slot):
                        act.wait_ge(s_z_sum, w.units(slot + 1))
                        if w.first > 0 or slot > 0:
                            act.wait_ge(s_h, w.units(slot))
                        nc.scalar.activation(z_gate[:], ps_z[:], ACT.Sigmoid, bias=rz_bias[:, 1:2]).then_inc(s_z, 1)
                    if w.prepares():
                        if slot == 0 and w.first >= 0:
                            adjt_hi_of(2)
                            adjt_hi_of(3)

            all_windows(window, act)

        @block.vector
        def _(dve):
            def low_part(dst, src, hi):
                return nc.vector.tensor_tensor(dst, src, raw(hi), ALU.subtract)

            dve.wait_ge(s_w0, 16)
            nc.vector.tensor_copy(w0_hi[:], w0_in[:]).then_inc(s_w0, 1)
            dve.wait_ge(s_w0, 17)
            low_part(w0_lo[:], w0_in[:], w0_hi[:]).then_inc(s_w0, 1)

            def weights():
                dve.wait_ge(s_small, 2 * 16)
                nc.vector.tensor_tensor(rz_bias[:], bih_cols[:, 0:2], bhh_cols[:, 0:2], ALU.add).then_inc(s_whh, 1)
                dve.wait_ge(s_weights, 3 * 16)
                nc.vector.tensor_copy(whh_hi[:], whh_t[:]).then_inc(s_whh, 1)
                dve.wait_ge(s_whh, 2)
                low_part(whh_lo[:], whh_t[:], whh_hi[:]).then_inc(s_whh, 1)
                for l in range(LAYERS):
                    dve.wait_ge(s_wc_hi, l + 1)
                    low_part(wc_lo[:, l, :], product_bank[l][:, 0:G * D], wc_hi[:, l, :]).then_inc(s_wc_lo, 1)

            def window(w):
                prev = w.units

                def xw_parts(half):
                    ps = ps_b[half][:].rearrange("p (c k d) -> p c k d", c=2, k=2)
                    if w.first == -1:
                        dve.wait_ge(s_bias0, 16)
                    dve.wait_ge(s_y_hi, w.prepared(2, half + 1))
                    low_part(y_lo[:, 2 * half:2 * half + 2, 0:D], ps[:, :, 1, :], y_hi[:, 2 * half:2 * half + 2, 0:D])
                    nc.vector.tensor_tensor(own[:, 2 * half:2 * half + 2, :], ps[:, :, 0, :],
                                            bias0[:].rearrange("p (o d) -> p o d", o=1).to_broadcast([P, 2, D]),
                                            ALU.add).then_inc(s_own, 1)

                def mean_parts():
                    dve.wait_ge(s_nsum_tok, w.prepared(1, 1))
                    dve.wait_ge(s_rinv, w.prepared(2, 2))
                    for c in range(C):
                        last = nc.vector.scalar_tensor_tensor(
                            out=mixed[:, c, :], in0=ps_b[0][:, c * D:(c + 1) * D],
                            scalar=row_inv[:, c:c + 1], in1=own[:, c, :], op0=ALU.mult, op1=ALU.add)
                    last.then_inc(s_mixed, 1)

                def residual():
                    dve.wait_ge(s_x_in, w.prepared(16, 16))
                    dve.wait_ge(s_mixed, w.prepared(1, 1))
                    nc.vector.scalar_tensor_tensor(out=pre1[:], in0=mixed[:], scalar=0.0, in1=x_in[:],
                                                   op0=ALU.max, op1=ALU.add).then_inc(s_pre1, 1)
                    dve.wait_ge(s_pre1, w.prepared(1, 1))

                def moments1():
                    for c in range(C):
                        nc.vector.bn_aggr(mv1[:, c, :], stats1[:, c, :]).then_inc(s_mv1, 1)
                    dve.wait_ge(s_mv1, w.prepared(C, C))
                    nc.vector.tensor_scalar(var1[:], mv1[:, :, 1], LN_EPS, None, ALU.add).then_inc(s_var1, 1)

                def stats1_of(cs):
                    for c in cs:
                        nc.vector.bn_stats(stats1[:, c, :], pre1[:, c, :]).then_inc(s_stats1, 1)

                def edges_of(cs):
                    for c in cs:
                        nc.vector.tensor_scalar(edges[:, bass.ds(ring, 1), c, :].rearrange("p o m -> p (o m)"),
                                                adj_in[:, c, :], 0.0, None, ALU.not_equal).then_inc(s_edges, 1)

                if w.prepares():
                    ring = dve.snap(w.batch(-1) % RING)
                if w.finishes():
                    kept = dve.snap(w.batch(3) % KEPT)

                for slot in range(SLOTS):
                    made = w.unit_before(slot)[1] + 1 if w.unit_before(slot) else None
                    if w.unit_before(slot):
                        dve.wait_ge(s_in_sum, w.units(slot))
                        dve.wait_ge(s_rhn, w.units(slot))
                        nc.vector.tensor_tensor(n_pre[:], ps_in[:], r_hn[:], ALU.add).then_inc(s_npre, 1)
                    if w.prepares():
                        if slot == 0:
                            dve.wait_ge(s_xt_hi, w.prepared(1, 1))
                            low_part(xt_lo[:], xt_in[:], xt_hi[:]).then_inc(s_xt_lo, 1)
                        if slot == 1:
                            xw_parts(1)
                        if slot == 3 and not w.ramps():
                            residual()
                            stats1_of((0, 1))
                        if slot == w.state_slot():
                            dve.wait_ge(s_rstd1, w.prepared(1, 1))
                            for c in range(C):
                                nc.vector.tensor_scalar(x1[:, c, :], pre1[:, c, :], mv1[:, c, 0:1],
                                                        rstd1[:, c:c + 1], ALU.subtract, ALU.mult).then_inc(s_x1, 1)
                    if w.unit_before(slot):
                        dve.wait_ge(s_n, w.units(slot))
                        nc.vector.scalar_tensor_tensor(out=zm1_n[:], in0=z_gate[:], scalar=1.0, in1=n_gate[:],
                                                       op0=ALU.subtract, op1=ALU.mult).then_inc(s_zm1n, 1)
                    if w.unit(slot):
                        dve.wait_ge(s_agg_hi, w.units(slot + 1))
                        low_part(agg_lo[:], ps_tok[:], agg_hi[:]).then_inc(s_agg_lo, 1)
                    if w.prepares() and slot == 3 and not w.ramps():
                        stats1_of((2, 3))
                        dve.wait_ge(s_stats1, w.prepared(C, C))
                    if w.unit_before(slot):
                        dve.wait_ge(s_zh, w.units(slot))
                        dve.wait_ge(s_zm1n, w.units(slot))
                        nc.vector.tensor_tensor(h[made][:], z_h[:], zm1_n[:], ALU.subtract).then_inc(s_h, 1)
                    if w.first == -1 and slot == 1:
                        weights()
                    if w.prepares():
                        if slot == 2:
                            mean_parts()
                        if slot == 3 and not w.ramps():
                            moments1()
                        if slot == 4 and not w.ramps():
                            dve.wait_ge(s_agg, w.units(LAST + 1))
                            edges_of(range(C))
                    if slot == 1 and w.finishes():
                        dve.wait_ge(s_last, w.finished(1, 1))
                        dve.wait_ge(s_x1_kept, w.finished(1, 1))
                        dve.wait_ge(s_cent2, w.freed())
                        b = w.batch(3)
                        for c in range(C):
                            last = nc.vector.scalar_tensor_tensor(
                                out=pre2[:, c, :], in0=ps_b[1][:, c * P:(c + 1) * P],
                                scalar=mask_cols[:, bass.ds(b * C + c, 1)],
                                in1=x1_kept[:, bass.ds(kept, 1), c, :].rearrange("p o d -> p (o d)"),
                                op0=ALU.mult, op1=ALU.add)
                        last.then_inc(s_end_read, 1)
                        dve.wait_ge(s_end_read, w.finished(1, 1))
                        for c in range(C):
                            nc.vector.bn_stats(stats2[:, c, :], pre2[:, c, :]).then_inc(s_stats2, 1)
                        dve.wait_ge(s_stats2, w.finished(C, C))
                    if w.prepares() and slot == 1:
                        dve.wait_ge(s_row_sum, w.prepared(C, C))
                        nc.vector.tensor_scalar(row_eps[:], row_sum[:], ROW_EPS, None, ALU.add).then_inc(s_rinv, 1)
                    if slot == 1 and w.finishes():
                        for c in range(C):
                            nc.vector.bn_aggr(mv2[:, c, :], stats2[:, c, :]).then_inc(s_mv2, 1)
                        dve.wait_ge(s_mv2, w.finished(C, C))
                        nc.vector.tensor_scalar(var2[:], mv2[:, :, 1], LN_EPS, None, ALU.add).then_inc(s_var2, 1)
                    if slot < 4 and w.unit(slot + 1):
                        dve.wait_ge(s_tok_hi, w.turned(slot + 2))
                        low_part(tok_lo[:], ps_tok[:], tok_hi[:]).then_inc(s_tok_lo, 1)
                    if w.prepares():
                        if slot == 0:
                            xw_parts(0)
                        if slot == 1:
                            dve.wait_ge(s_rinv, w.prepared(2, 1))
                            nc.vector.reciprocal(row_inv[:], row_eps[:]).then_inc(s_rinv, 1)
                    if w.prepares() and slot == 2 and w.ramps():
                        residual()
                        stats1_of(range(C))
                        dve.wait_ge(s_stats1, w.prepared(C, C))
                        moments1()
                    if w.unit(slot):
                        dve.wait_ge(s_r, w.units(slot + 1))
                        nc.vector.scalar_tensor_tensor(out=r_hn[:], in0=ps_hn[:], scalar=bhh_cols[:, 2:3],
                                                       in1=r_gate[:], op0=ALU.add, op1=ALU.mult).then_inc(s_rhn, 1)
                    if w.prepares() and slot == 1 and w.ramps():
                        edges_of(range(C))

            all_windows(window, dve)

        @block.tensor
        def _(pe):
            def turn(dst, src):
                return nc.tensor.transpose(dst, src, ident[:])

            def split_product(dst, lhs_hi, lhs_lo, rhs_hi, rhs_lo, start, stop):
                nc.tensor.matmul(dst, lhs_hi, rhs_hi, start=start, stop=False)
                nc.tensor.matmul(dst, lhs_hi, rhs_lo, start=False, stop=False)
                return nc.tensor.matmul(dst, lhs_lo, rhs_hi, start=False, stop=stop)

            def weights():
                pe.wait_ge(s_weights, 3 * 16)
                for l in range(LAYERS):
                    nc.tensor.matmul(product_bank[l][:, 0:G * D], wl_t[:, l, :], wih_t[:],
                                     start=True, stop=True).then_inc(s_w_prod, 1)

            pe.wait_ge(s_const, 3)
            pe.wait_ge(s_w0, 18)

            def window(w):

                def own_products(half):
                    for c in range(2):
                        ts = slice((2 * half + c) * P, (2 * half + c + 1) * P)
                        last = split_product(ps_b[half][:, c * 2 * D:(c + 1) * 2 * D], xt_hi[:, ts], xt_lo[:, ts],
                                             w0_hi[:], w0_lo[:], True, True)
                    last.then_inc(s_xw, 1)

                def neighbour_sums(js):
                    for j in js:
                        pe.wait_ge(s_adjt_lo, w.prepared(C, j + 1))
                        last = split_product(ps_b[2][:], y_hi[:, j, :], y_lo[:, j, :], adjt_hi[:, j, :],
                                             adjt_lo[:, j, :], j == 0, j == C - 1)
                    return last

                def gate(dst, g, hi, lo, weights_hi, weights_lo, start, stop):
                    gs = slice(g * D, (g + 1) * D)
                    return split_product(dst[:], weights_hi[:, gs], weights_lo[:, gs], hi[:], lo[:], start, stop)

                ring = [pe.snap(w.batch(back) % RING) if w.first - back >= 0 else None for back in range(RING)]

                def edges_from(c, back):
                    return edges[:, bass.ds(ring[back], 1), c, :].rearrange("p o m -> p (o m)")

                for slot in range(SLOTS):
                    unit = w.unit(slot)
                    layer = w.unit(slot)[1] if w.unit(slot) else None
                    if unit:
                        if layer == 0:
                            if w.first == 0:
                                pe.wait_ge(s_wc_lo, LAYERS)
                            pe.wait_ge(s_edges, w.young(C, C))
                            pe.wait_ge(s_x1_hi, w.young(1, 1))
                        else:
                            pe.wait_ge(s_tok_lo, w.turned(slot + 1))
                        for c in range(C):
                            nc.tensor.matmul(ps_tok[:], tok_hi[:, c * P:(c + 1) * P], edges_from(c, unit[0]),
                                             start=c == 0, stop=False)
                        if layer == 0:
                            pe.wait_ge(s_x1_lo, w.young(1, 1))
                        for c in range(C):
                            last = nc.tensor.matmul(ps_tok[:], tok_lo[:, c * P:(c + 1) * P],
                                                    edges_from(c, unit[0]), start=False, stop=c == C - 1)
                        last.then_inc(s_agg, 1)
                    if w.first == -1 and slot == 1:
                        weights()
                    if w.prepares():
                        if slot == 1:
                            pe.wait_ge(s_own, w.prepared(2, 1))
                            if w.first >= 0:
                                pe.wait_ge(s_nsum_out, w.prepared(1, 0))
                            neighbour_sums((0, 1))
                        if slot == 2:
                            pe.wait_ge(s_nsum_out, w.prepared(1, 1))
                            for c in range(C):
                                last = turn(ps_b[0][:, c * P:(c + 1) * P], mean_t[:, c * P:(c + 1) * P])
                            last.then_inc(s_nsum_tok, 1)
                    if slot == 1 and w.finishes():
                        if w.prepares():
                            pe.wait_ge(s_own, w.prepared(2, 2))
                        pe.wait_ge(s_h, w.last_layers())
                        for c in range(C):
                            last = turn(ps_b[1][:, c * P:(c + 1) * P], h[LAYERS][:, c * P:(c + 1) * P])
                        last.then_inc(s_last, 1)
                    if unit:
                        if slot == 0:
                            if w.first == 0:
                                pe.wait_ge(s_wc_lo, LAYERS)
                                pe.wait_ge(s_whh, 3)
                            pe.wait_ge(s_h0_lo, w.young(1, 1))
                        else:
                            pe.wait_ge(s_h_lo, w.until_made(slot, range(LAYERS - 1)))
                        started = w.first > 0 or slot > 0
                        if started:
                            pe.wait_ge(s_rhn, w.units(slot))
                        gate(ps_hn, 2, h_hi[layer], h_lo[layer], whh_hi, whh_lo, True, True)
                        if started:
                            pe.wait_ge(s_z, w.units(slot))
                        gate(ps_r, 0, h_hi[layer], h_lo[layer], whh_hi, whh_lo, True, False)
                        gate(ps_z, 1, h_hi[layer], h_lo[layer], whh_hi, whh_lo, True, False)
                    if w.prepares() and slot == w.state_slot():
                        pe.wait_ge(s_x1, w.prepared(C, C))
                        if w.finishes():
                            pe.wait_ge(s_end_read, w.finished(1, 1))
                        for c in range(C):
                            last = turn(ps_b[1][:, c * P:(c + 1) * P], x1[:, c, :])
                        last.then_inc(s_x1t, 1)
                    if unit:
                        pe.wait_ge(s_agg_lo, w.units(slot + 1))
                    if slot < 4 and w.unit(slot + 1):
                        t = w.unit(slot + 1)[1]
                        pe.wait_ge(s_h, w.until_made(slot + 1))
                        for c in range(C):
                            last = turn(ps_tok[:, c * P:(c + 1) * P], h[t][:, c * P:(c + 1) * P])
                        last.then_inc(s_tok, 1)
                    if w.prepares():
                        if slot == 0:
                            pe.wait_ge(s_xt_lo, w.prepared(1, 1))
                            if w.first >= 0:
                                pe.wait_ge(s_mixed, w.prepared(1, 0))
                                pe.wait_ge(s_h0, w.prepared(1, 0))
                            own_products(0)
                            own_products(1)
                        if slot == 1:
                            pe.wait_ge(s_own, w.prepared(2, 2))
                            neighbour_sums((2, 3)).then_inc(s_nsum, 1)
                    if unit:
                        wi_hi, wi_lo = wc_hi[:, layer, :], wc_lo[:, layer, :]
                        gate(ps_r, 0, agg_hi, agg_lo, wi_hi, wi_lo, False, True).then_inc(s_r_sum, 1)
                        gate(ps_z, 1, agg_hi, agg_lo, wi_hi, wi_lo, False, True).then_inc(s_z_sum, 1)
                        if started:
                            pe.wait_ge(s_npre, w.units(slot))
                        gate(ps_in, 2, agg_hi, agg_lo, wi_hi, wi_lo, True, True).then_inc(s_in_sum, 1)

            all_windows(window, pe)


def kernel(x, adj, nodemask, L0_gnn_weight, L0_gnn_bias, L1_gnn_weight, L1_gnn_w_ih, L1_gnn_w_hh, L1_gnn_b_ih,
           L1_gnn_b_hh):
    import numpy as _np
    import concourse.bacc as _bacc
    from concourse import mybir as _mybir
    from concourse.bass_utils import run_bass_kernel_spmd as _run

    x, adj, nodemask = _np.asarray(x), _np.asarray(adj), _np.asarray(nodemask)
    batches, nodes = nodemask.shape
    laid_out = {
        "x": x,
        "x_t": x.transpose(0, 2, 1),
        "adj": adj,
        "adj_t": adj.transpose(0, 2, 1),
        "mask": nodemask.reshape(batches * nodes // P, P).transpose(1, 0),
        "w0": _np.asarray(L0_gnn_weight),
        "b0": _np.asarray(L0_gnn_bias),
        "wl_t": _np.asarray(L1_gnn_weight).transpose(0, 2, 1),
        "w_ih_t": _np.asarray(L1_gnn_w_ih).transpose(1, 0),
        "w_hh_t": _np.asarray(L1_gnn_w_hh).transpose(1, 0),
        "gru_b": _np.stack([_np.asarray(L1_gnn_b_ih), _np.asarray(L1_gnn_b_hh)]).reshape(6, P).transpose(1, 0),
    }
    nc = _bacc.Bacc("TRN2", target_bir_lowering=False, num_devices=1)
    arrays, args = {}, []
    for name, a in laid_out.items():
        a = _np.ascontiguousarray(a)
        arrays[f"in_{name}_dram"] = a
        args.append(nc.dram_tensor(f"in_{name}_dram", a.shape, _mybir.dt.from_np(a.dtype), kind="ExternalInput").ap())
    args.append(nc.dram_tensor("out_dram", x.shape, _mybir.dt.float32, kind="ExternalOutput").ap())
    program(nc, *args)
    return _run(nc, [arrays], core_ids=[0]).results[0]["out_dram"]
```
